# Optimizing a Trainium2 kernel written in Bass

```python
import numpy as np
import jax
import jax.numpy as jnp

def _softmax(x, axis=-1):
    return jax.nn.softmax(x, axis=axis)

def _gelu(x):
    return jax.nn.gelu(x, approximate=True)

def _silu(x):
    return jax.nn.silu(x)

def _sigmoid(x):
    return jax.nn.sigmoid(x)

def _layernorm(x, axis=-1, eps=1e-05):
    m = jnp.mean(x, axis=axis, keepdims=True)
    v = jnp.var(x, axis=axis, keepdims=True)
    return (x - m) / jnp.sqrt(v + eps)

def _scatter_add(tgt, idx, src, axis=0):
    return tgt.at[idx].add(src)

def _segment_sum(src, seg, n):
    return jax.ops.segment_sum(src, seg, n)
kernel_name = 'mk_gnn_ffn_d1_gnn_r8_a861ad'

def setup_inputs(seed: int=0):
    np.random.seed(seed)
    _w = jnp.asarray

    def _rec_inputs():
        import jax
        import jax.numpy as jnp
        _gk = jax.random.key(seed)
        x = -0.0003713 + 1 * jax.random.normal(jax.random.fold_in(_gk, 1), (6250, 256), jnp.float32)
        _s = jax.random.randint(jax.random.fold_in(_gk, 2), (100000,), 0, 6250, jnp.int32)
        _d = jax.random.randint(jax.random.fold_in(_gk, 3), (100000,), 0, 6250, jnp.int32)
        _loop = jnp.arange(6250, dtype=jnp.int32)
        src = jnp.concatenate([_s, _d, _loop])
        dst = jnp.concatenate([_d, _s, _loop])
        _o = jnp.argsort(dst, stable=True)
        src = src[_o]
        dst = dst[_o]
        edge_weight1 = jax.random.uniform(jax.random.fold_in(_gk, 12), (206250, 1), jnp.float32, 0.0, 0.999999)
        return (x, src, dst, edge_weight1)
    x, src, dst, edge_weight1 = _rec_inputs()

    def _L0_gnn_setup():
        import jax, jax.numpy as jnp
        import numpy as np
        N_NODES = 6250
        N_EDGES = 100000
        DIM = 256
        key = jax.random.key(seed)
        ks = jax.random.split(key, 8)
        x = jax.random.normal(ks[0], (N_NODES, DIM), dtype=jnp.float32)
        row = jax.random.randint(ks[1], (N_EDGES,), 0, N_NODES)
        col = jax.random.randint(ks[2], (N_EDGES,), 0, N_NODES)
        col = jnp.where(col == row, (col + 1) % N_NODES, col)
        edge_index = jnp.stack([row, col]).astype(jnp.int64)
        edge_weight = jax.random.uniform(ks[3], (N_EDGES, 1), dtype=jnp.float32)
        bound = 1.0 / np.sqrt(DIM)
        W1 = jax.random.uniform(ks[4], (DIM, DIM), minval=-bound, maxval=bound, dtype=jnp.float32)
        b1 = jax.random.uniform(ks[5], (DIM,), minval=-bound, maxval=bound, dtype=jnp.float32)
        W2 = jax.random.uniform(ks[6], (DIM, DIM), minval=-bound, maxval=bound, dtype=jnp.float32)
        b2 = jax.random.uniform(ks[7], (DIM,), minval=-bound, maxval=bound, dtype=jnp.float32)
        return {'x': x, 'edge_index': edge_index, 'edge_weight': edge_weight, 'W1': W1, 'b1': b1, 'W2': W2, 'b2': b2}
    _L0_gnn_all = _L0_gnn_setup()
    _L0_gnn_in = {k: v for k, v in _L0_gnn_all.items() if k in ('W1', 'b1', 'W2', 'b2')}
    del _L0_gnn_all

    def _L0_ffn_setup():
        import jax, jax.numpy as jnp
        import numpy as np
        NUM_EXPERTS = 8
        TOP_K = 2
        B, S, D = (8, 1024, 256)

        def _moe(tokens, router_w, w1, b1, w2, b2):
            N = tokens.shape[0]
            E = router_w.shape[0]
            logits = tokens.astype(jnp.float32) @ router_w.astype(jnp.float32).T
            probs = jax.nn.softmax(logits, axis=-1)
            rw, re = jax.lax.top_k(probs, TOP_K)
            if TOP_K > 1:
                rw = rw / jnp.maximum(rw.sum(-1, keepdims=True), 1e-12)
            rw = rw.astype(tokens.dtype)
            combine = jnp.zeros((N, E), tokens.dtype).at[jnp.arange(N)[:, None], re].set(rw)
            out = tokens
            for e in range(E):
                h = jax.nn.gelu(tokens @ w1[e] + b1[e], approximate=False)
                y = h @ w2[e] + b2[e]
                out = out + combine[:, e:e + 1] * y
            return out
        key = jax.random.key(seed)
        ks = jax.random.split(key, 4)
        scale = 1.0 / np.sqrt(D).astype(np.float32)
        return {'input_embeddings': jax.random.normal(ks[0], (B, S, D), jnp.float32), 'router_w': jax.random.normal(ks[1], (NUM_EXPERTS, D), jnp.float32) * scale, 'w1': jax.random.normal(ks[2], (NUM_EXPERTS, D, D), jnp.float32) * scale, 'b1': jnp.zeros((NUM_EXPERTS, D), jnp.float32), 'w2': jax.random.normal(ks[3], (NUM_EXPERTS, D, D), jnp.float32) * scale, 'b2': jnp.zeros((NUM_EXPERTS, D), jnp.float32)}
    _L0_ffn_all = _L0_ffn_setup()
    _L0_ffn_in = {k: v for k, v in _L0_ffn_all.items() if k in ('router_w', 'w1', 'b1', 'w2', 'b2')}
    del _L0_ffn_all
    return {'x': x, 'src': src, 'dst': dst, 'edge_weight1': edge_weight1, 'L0_gnn_W1': _L0_gnn_in['W1'], 'L0_gnn_b1': _L0_gnn_in['b1'], 'L0_gnn_W2': _L0_gnn_in['W2'], 'L0_gnn_b2': _L0_gnn_in['b2'], 'L0_ffn_router_w': _L0_ffn_in['router_w'], 'L0_ffn_w1': _L0_ffn_in['w1'], 'L0_ffn_b1': _L0_ffn_in['b1'], 'L0_ffn_w2': _L0_ffn_in['w2'], 'L0_ffn_b2': _L0_ffn_in['b2']}

def reference(x, src, dst, edge_weight1, L0_gnn_W1, L0_gnn_b1, L0_gnn_W2, L0_gnn_b2, L0_ffn_router_w, L0_ffn_w1, L0_ffn_b1, L0_ffn_w2, L0_ffn_b2):
    import jax
    import jax.numpy as jnp

    def _L0_gnn_ref(x, edge_index, edge_weight, W1, b1, W2, b2):
        import jax, jax.numpy as jnp
        import numpy as np
        N_NODES = 6250
        N_EDGES = 100000
        DIM = 256
        n = x.shape[0]
        loops = jnp.arange(n)
        row = jnp.concatenate([edge_index[0], loops])
        col = jnp.concatenate([edge_index[1], loops])
        ew = jnp.concatenate([edge_weight, jnp.ones((n, 1), x.dtype)], axis=0)
        deg = jnp.zeros((n,), x.dtype).at[col].add(1.0)
        dinv = jnp.where(deg > 0, deg ** (-0.5), 0.0)[:, None]
        norm = dinv[row] * ew * dinv[col]

        def gcn_layer(h, W, b):
            h = h @ W.T + b
            msg = norm * h[row]
            out = jax.ops.segment_sum(msg, col, num_segments=n)
            return jax.nn.relu(out)
        h = gcn_layer(x, W1, b1)
        h = gcn_layer(h, W2, b2)
        return h

    def _L0_ffn_ref(input_embeddings, router_w, w1, b1, w2, b2):
        import jax, jax.numpy as jnp
        import numpy as np
        NUM_EXPERTS = 8
        TOP_K = 2
        B, S, D = (8, 1024, 256)

        def _moe(tokens, router_w, w1, b1, w2, b2):
            N = tokens.shape[0]
            E = router_w.shape[0]
            logits = tokens.astype(jnp.float32) @ router_w.astype(jnp.float32).T
            probs = jax.nn.softmax(logits, axis=-1)
            rw, re = jax.lax.top_k(probs, TOP_K)
            if TOP_K > 1:
                rw = rw / jnp.maximum(rw.sum(-1, keepdims=True), 1e-12)
            rw = rw.astype(tokens.dtype)
            combine = jnp.zeros((N, E), tokens.dtype).at[jnp.arange(N)[:, None], re].set(rw)
            out = tokens
            for e in range(E):
                h = jax.nn.gelu(tokens @ w1[e] + b1[e], approximate=False)
                y = h @ w2[e] + b2[e]
                out = out + combine[:, e:e + 1] * y
            return out
        b, s, d = input_embeddings.shape
        tokens = input_embeddings.reshape(b * s, d)
        return _moe(tokens, router_w, w1, b1, w2, b2).reshape(b, s, d)
    edge_index = jnp.stack([src, dst])
    x = x + _L0_gnn_ref(_layernorm(x, axis=-1), edge_index, edge_weight1, L0_gnn_W1, L0_gnn_b1, L0_gnn_W2, L0_gnn_b2)
    x = x + _L0_ffn_ref(_layernorm(x, axis=-1)[None], L0_ffn_router_w, L0_ffn_w1, L0_ffn_b1, L0_ffn_w2, L0_ffn_b2)[0]
    return x

_drawn_inputs = setup_inputs


def setup_inputs(seed=0):
    import zlib

    import numpy as np

    out = dict(_drawn_inputs(seed))
    spreads = {'L0_ffn_b1': (0.0, 2.0), 'L0_ffn_b2': (0.0, 0.8)}
    factors = {'edge_weight1': 8.0,
     'L0_gnn_W1': 7.072,
     'L0_gnn_b1': 8.0,
     'L0_gnn_W2': 4.458,
     'L0_gnn_b2': 2.829}
    for name, (base, spread) in spreads.items():
        noise = np.random.default_rng([zlib.crc32(name.encode()), seed]).standard_normal(out[name].shape)
        drawn = base * np.exp(spread * noise) if base else spread * noise
        out[name] = jnp.asarray(drawn.astype(out[name].dtype))
    for name, factor in factors.items():
        out[name] = (out[name] * factor).astype(out[name].dtype)
    return out
```

```python
import concourse.bass as bass
from concourse import mybir
from contextlib import ExitStack

F32 = mybir.dt.float32
BF16 = mybir.dt.bfloat16
I32 = mybir.dt.int32
ALU = mybir.AluOpType
ACT = mybir.ActivationFunctionType
AX = mybir.AxisListType.X

P = 128
D = 256
HALF = D // P
N_NODES = 6250
N_EDGES = 206250
EXPERTS = 8
TILES = -(-N_NODES // P)
NODES = TILES * P
TILES_PAD = TILES + 1
GROUP = 11
GROUPS_PER_STEP = 3
STEPS = TILES
CHUNKS_PER_STEP = GROUP * GROUPS_PER_STEP
CHUNKS = STEPS * CHUNKS_PER_STEP
GROUPS = STEPS * GROUPS_PER_STEP
CHUNKS_PAD = CHUNKS + GROUP
assert CHUNKS * P >= N_EDGES
WINDOW = 64
AGG = TILES_PAD * P
LO = 64
HI = NODES // LO
BATCH = 7
PASSES = TILES // BATCH
assert BATCH * PASSES == TILES and HI * LO == NODES and HI == 2 * TILES
EPS = 1e-5
RMAX = bass.bass_isa.ReduceOp.max


def gnn_ffn_kernel(nc, x, src, dst, weight, gnn_w1, gnn_b1, gnn_w2, gnn_b2,
                   router, moe_w1, moe_b1, moe_w2, moe_b2, out):
    ctx = ExitStack()
    with ctx:
        def sb(name, shape, dt=F32):
            return ctx.enter_context(nc.sbuf_tensor(name, shape, dt))

        def sem(name):
            return ctx.enter_context(nc.semaphore(name))

        table = nc.dram_tensor("table", [NODES, D], F32, kind="Internal").ap()
        table_tiles = table.rearrange("(t p) d -> p t d", p=P)
        x_tiles = x.rearrange("(t p) d -> p t d", p=P)
        out_tiles = out.rearrange("(t p) d -> p t d", p=P)

        rows = sb("rows", [P, TILES, D])
        ring = rows[:, 0:CHUNKS_PER_STEP, :]
        dst_f = sb("dst_f", [P, CHUNKS_PAD])
        dst_rel = sb("dst_rel", [P, CHUNKS_PAD])
        w_edge = sb("w_edge", [P, CHUNKS_PAD])
        idx = sb("idx", [P, GROUPS_PER_STEP, GROUP], I32)
        base_f = sb("base_f", [P, GROUPS + 1])
        base_i = sb("base_i", [P, GROUPS + 1], I32)
        rounds_i = sb("rounds_i", [P, 2], I32)
        iota = sb("iota", [P, P])
        ident = sb("ident", [P, P])
        w1_sb = sb("w1_sb", [P, HALF, D])
        w2_sb = sb("w2_sb", [P, HALF, D])
        b1_sb = sb("b1_sb", [P, D])
        b2_sb = sb("b2_sb", [P, D])
        router_sb = sb("router_sb", [P, HALF, EXPERTS])
        moe_w1_sb = sb("moe_w1_sb", [P, EXPERTS, HALF, D])
        moe_w2_sb = sb("moe_w2_sb", [P, EXPERTS, HALF, D])
        moe_b1_sb = sb("moe_b1_sb", [P, EXPERTS * HALF])
        moe_b2_sb = sb("moe_b2_sb", [EXPERTS, D])
        eps = sb("eps", [P, 1])
        dinv = sb("dinv", [P, TILES_PAD])
        buf_a = sb("buf_a", [P, BATCH, D])
        buf_b = sb("buf_b", [P, BATCH, D])

        bank = [ctx.enter_context(nc.psum_tensor(f"bank{i}", [P, 512], F32)) for i in range(8)]

        bc = lambda ap, shape: ap.to_broadcast(shape)

        setup_ctx = ExitStack()

        def tmp(name, shape, dt=F32):
            return setup_ctx.enter_context(nc.sbuf_tensor(name, shape, dt))

        dst_i = tmp("dst_i", [P, CHUNKS_PAD], I32)
        lo_i = tmp("lo_i", [P, CHUNKS_PAD], I32)
        lo_b = tmp("lo_b", [P, CHUNKS_PAD], BF16)
        hi_b = tmp("hi_b", [P, CHUNKS_PAD], BF16)
        onehot_lo = tmp("onehot_lo", [P, GROUPS_PER_STEP, GROUP, LO], BF16)
        onehot_hi = tmp("onehot_hi", [P, GROUPS_PER_STEP, GROUP, HI], BF16)
        extent = tmp("extent", [P, 2, GROUPS + 1])
        extent_all = tmp("extent_all", [P, 2, GROUPS + 1])
        span = tmp("span", [P, GROUPS + 1])
        span_max = tmp("span_max", [P, 1])
        iota_lo = tmp("iota_lo", [P, LO], BF16)
        iota_hi = tmp("iota_hi", [P, HI], BF16)
        zeros = tmp("zeros", [P, P], BF16)
        deg_lohi = tmp("deg_lohi", [LO, TILES, 2])
        deg = tmp("deg", [P, TILES])
        deg_root = tmp("deg_root", [P, TILES])
        stats = tmp("stats", [P, TILES, 6])
        mean = tmp("mean", [P, TILES])
        var = tmp("var", [P, TILES])
        gap = tmp("gap", [P, TILES])
        rstd = tmp("rstd", [P, TILES])
        shift = tmp("shift", [P, TILES])

        s_edge = sem("edges_loaded")
        s_wt = sem("weights_loaded")
        s_x = [sem(f"x_loaded{i}") for i in range(PASSES)]
        s_const = sem("constants_ready")
        s_split = sem("dst_split")
        s_extent = sem("extent_ready")
        s_extent_all = sem("extent_reduced")
        s_hot = sem("onehots_ready")
        s_hot_used = sem("onehots_used")
        s_deg = sem("degree_counted")
        s_deg_sb = sem("degree_copied")
        s_deg_tile = sem("degree_by_tile")
        s_root = sem("degree_root")
        s_dinv = sem("dinv_ready")
        s_var = sem("variance_ready")
        s_std = sem("deviation_ready")
        s_norm = sem("norm_factors_ready")
        s_xn = sem("normalised_rows")
        s_xn_t = sem("rows_transposed")
        s_xt = sem("transposed_copied")
        s_h = sem("h_matmul")
        s_rows = sem("h_rows_ready")
        s_chain_v = sem("vector_step")
        s_chain_g = sem("gpsimd_step")

        with nc.Block() as block:
            @block.sync
            def _(sp):
                sp.dma_start(dst_i[:], dst).then_inc(s_edge, 16)
                for i in range(PASSES):
                    t = slice(i * BATCH, (i + 1) * BATCH)
                    sp.dma_start(rows[:, t, :], x_tiles[:, t, :]).then_inc(s_x[i], 16)
                sp.dma_start(w_edge[:], weight).then_inc(s_wt, 16)
                sp.wait_ge(s_deg_sb, 1)
                for odd in range(2):
                    with nc.allow_non_contiguous_dma(reason="49 degrees per partition"):
                        sp.dma_start(deg[odd * LO:(odd + 1) * LO, :], deg_lohi[:, :, odd]).then_inc(s_deg_tile, 16)
                sp.wait_ge(s_wt, 16)

            @block.scalar
            def _(act):
                act.dma_start(w1_sb[:], gnn_w1.rearrange("(k p) n -> p k n", p=P)).then_inc(s_wt, 16)
                act.dma_start(b1_sb[:], gnn_b1.partition_broadcast(P)).then_inc(s_wt, 16)
                act.dma_start(w2_sb[:], gnn_w2.rearrange("(k p) n -> p k n", p=P)).then_inc(s_wt, 16)
                act.dma_start(b2_sb[:], gnn_b2.partition_broadcast(P)).then_inc(s_wt, 16)
                act.dma_start(router_sb[:], router.rearrange("(k p) n -> p k n", p=P)).then_inc(s_wt, 16)
                act.dma_start(moe_w1_sb[:], moe_w1.rearrange("e (k p) n -> p e k n", p=P)).then_inc(s_wt, 16)
                act.dma_start(moe_w2_sb[:], moe_w2.rearrange("e (k p) n -> p e k n", p=P)).then_inc(s_wt, 16)
                act.dma_start(moe_b1_sb[:], moe_b1).then_inc(s_wt, 16)
                act.dma_start(moe_b2_sb[:], moe_b2).then_inc(s_wt, 16)
                act.wait_ge(s_const, 6)
                act.wait_ge(s_var, 1)
                nc.scalar.activation(rstd[:], var[:], ACT.Sqrt, bias=eps[:, 0:1]).then_inc(s_std, 1)
                act.wait_ge(s_norm, 1)
                with act.Fori(0, PASSES) as it:
                    for j in range(BATCH):
                        t = it * BATCH + j
                        act.wait_ge(s_xt, t + 1)
                        nc.scalar.activation(buf_a[:, j, :], rows[:, bass.ds(t, 1), :], ACT.Identity,
                                             scale=rstd[:, bass.ds(t, 1)],
                                             bias=shift[:, bass.ds(t, 1)]).then_inc(s_xn, 1)
                act.wait_ge(s_deg_tile, 32)
                nc.scalar.activation(deg_root[:], deg[:], ACT.Sqrt, bias=1.0).then_inc(s_root, 1)

            @block.gpsimd
            def _(pool):
                def step(ins, n):
                    ins.then_inc(s_chain_g, 1)
                    pool.wait_ge(s_chain_g, n)
                nc.gpsimd.iota(iota[:], pattern=[[1, P]], base=0, channel_multiplier=0,
                               allow_small_or_imprecise_dtypes=True).then_inc(s_const, 1)
                nc.gpsimd.iota(iota_lo[:], pattern=[[1, LO]], base=0, channel_multiplier=0,
                               allow_small_or_imprecise_dtypes=True).then_inc(s_const, 1)
                nc.gpsimd.iota(iota_hi[:], pattern=[[1, HI]], base=0, channel_multiplier=0,
                               allow_small_or_imprecise_dtypes=True).then_inc(s_const, 1)
                nc.gpsimd.memset(zeros[:], 0.0).then_inc(s_const, 1)
                nc.gpsimd.memset(eps[:], EPS).then_inc(s_const, 1)
                step(nc.gpsimd.memset(ident[:], 0.0), 1)
                nc.gpsimd.affine_select(out=ident[:], in_=ident[:], compare_op=ALU.not_equal, fill=1.0,
                                        base=0, pattern=[[-1, P]], channel_multiplier=1).then_inc(s_const, 1)
                pool.wait_ge(s_extent, 2)
                nc.gpsimd.partition_all_reduce(extent_all[:].rearrange("p a g -> p (a g)"),
                                               extent[:].rearrange("p a g -> p (a g)"), P, RMAX)\
                    .then_inc(s_extent_all, 1)

            @block.vector
            def _(dve):
                chain = [0]

                def step(ins):
                    chain[0] += 1
                    ins.then_inc(s_chain_v, 1)
                    dve.wait_ge(s_chain_v, chain[0])

                def norm_stats():
                    for i in range(PASSES):
                        dve.wait_ge(s_x[i], 16)
                    with dve.Fori(0, TILES) as t:
                        nc.vector.bn_stats(stats[:, bass.ds(t, 1), :].rearrange("p a b -> p (a b)"),
                                           rows[:, bass.ds(t, 1), :].rearrange("p a b -> p (a b)"))\
                            .then_inc(s_chain_v, 1)
                    chain[0] += TILES
                    dve.wait_ge(s_chain_v, chain[0])
                    st = lambda k: stats[:, :, k]
                    nc.vector.tensor_tensor(mean[:], st(1), st(4), ALU.add).then_inc(s_chain_v, 1)
                    nc.vector.tensor_tensor(gap[:], st(1), st(4), ALU.subtract).then_inc(s_chain_v, 1)
                    nc.vector.tensor_tensor(var[:], st(2), st(5), ALU.add).then_inc(s_chain_v, 1)
                    chain[0] += 3
                    dve.wait_ge(s_chain_v, chain[0])
                    step(nc.vector.tensor_tensor(gap[:], gap[:], gap[:], ALU.mult))
                    nc.vector.tensor_scalar(mean[:], mean[:], 0.5, None, ALU.mult).then_inc(s_chain_v, 1)
                    nc.vector.tensor_scalar(var[:], var[:], 1.0 / D, None, ALU.mult).then_inc(s_chain_v, 1)
                    chain[0] += 2
                    dve.wait_ge(s_chain_v, chain[0])
                    nc.vector.scalar_tensor_tensor(var[:], gap[:], 0.25, var[:], ALU.mult, ALU.add).then_inc(s_var, 1)
                    dve.wait_ge(s_std, 1)
                    step(nc.vector.reciprocal(rstd[:], rstd[:]))
                    nc.vector.scalar_tensor_tensor(shift[:], mean[:], -1.0, rstd[:], ALU.mult, ALU.mult)\
                        .then_inc(s_norm, 1)

                dve.wait_ge(s_edge, 16)
                nc.vector.tensor_copy(dst_f[:], dst_i[:]).then_inc(s_chain_v, 1)
                nc.vector.tensor_scalar(lo_i[:], dst_i[:], LO - 1, None, ALU.bitwise_and).then_inc(s_chain_v, 1)
                chain[0] += 2
                dve.wait_ge(s_chain_v, chain[0])
                step(nc.vector.tensor_copy(lo_b[:], lo_i[:]))
                step(nc.vector.tensor_scalar(lo_i[:], dst_i[:], LO.bit_length() - 1, None, ALU.logical_shift_right))
                nc.vector.tensor_copy(hi_b[:], lo_i[:]).then_inc(s_split, 1)
                by_group = dst_f[:].rearrange("p (g c) -> p g c", c=GROUP)
                nc.vector.tensor_reduce(extent[:, 0, :], by_group, AX, ALU.min, negate=True).then_inc(s_extent, 1)
                nc.vector.tensor_reduce(extent[:, 1, :], by_group, AX, ALU.max).then_inc(s_extent, 1)
                norm_stats()

                dve.wait_ge(s_const, 6)
                dve.wait_ge(s_split, 1)
                with dve.Fori(0, STEPS) as it:
                    for j in range(GROUPS_PER_STEP):
                        g = it * GROUPS_PER_STEP + j
                        dve.wait_ge(s_hot_used, g + 1)
                        c = it * CHUNKS_PER_STEP + j * GROUP
                        nc.vector.tensor_tensor(
                            onehot_lo[:, j], bc(iota_lo[:].unsqueeze(1), [P, GROUP, LO]),
                            bc(lo_b[:, bass.ds(c, GROUP)].unsqueeze(2), [P, GROUP, LO]), ALU.is_equal)\
                            .then_inc(s_hot, 1)
                        nc.vector.tensor_tensor(
                            onehot_hi[:, j], bc(iota_hi[:].unsqueeze(1), [P, GROUP, HI]),
                            bc(hi_b[:, bass.ds(c, GROUP)].unsqueeze(2), [P, GROUP, HI]), ALU.is_equal)\
                            .then_inc(s_hot, 1)

                dve.wait_ge(s_wt, 160)
                with dve.Fori(0, PASSES) as it:
                    for j in range(BATCH):
                        t = it * BATCH + j
                        dve.wait_ge(s_xn_t, t + 1)
                        nc.vector.tensor_copy(buf_b[:, j, :], bank[1 + j % 2][:, 0:D]).then_inc(s_xt, 1)
                        dve.wait_ge(s_h, t + 1)
                        nc.vector.tensor_tensor(rows[:, bass.ds(t, 1), :].rearrange("p a b -> p (a b)"),
                                                bank[3 + j % 2][:, 0:D], b1_sb[:], ALU.add).then_inc(s_rows, 1)

                dve.wait_ge(s_deg, 1)
                nc.vector.tensor_copy(deg_lohi[:], bank[0][0:LO, 0:HI].rearrange("p (t o) -> p t o", o=2))\
                    .then_inc(s_deg_sb, 1)
                dve.wait_ge(s_root, 1)
                nc.vector.memset(dinv[:, TILES:TILES_PAD], 1.0).then_inc(s_dinv, 1)
                nc.vector.reciprocal(dinv[:, 0:TILES], deg_root[:]).then_inc(s_dinv, 1)

                dve.wait_ge(s_extent_all, 1)
                nc.vector.tensor_tensor(span[:], extent_all[:, 0, :], extent_all[:, 1, :], ALU.add)\
                    .then_inc(s_chain_v, 1)
                nc.vector.tensor_scalar(base_f[:], extent_all[:, 0, :], -1.0, None, ALU.mult)\
                    .then_inc(s_chain_v, 1)
                chain[0] += 2
                dve.wait_ge(s_chain_v, chain[0])
                step(nc.vector.tensor_reduce(span_max[:], span[:, 0:GROUPS], AX, ALU.max))
                step(nc.vector.tensor_copy(rounds_i[:, 0:1], span_max[:]))
                step(nc.vector.tensor_scalar(rounds_i[:, 1:2], rounds_i[:, 0:1], WINDOW.bit_length() - 1, None,
                                             ALU.logical_shift_right))
                step(nc.vector.tensor_scalar(rounds_i[:, 0:1], rounds_i[:, 1:2], 1.0, None, ALU.add))

            @block.tensor
            def _(pe):
                pe.sem_inc(s_hot_used, GROUPS_PER_STEP)
                pe.wait_ge(s_const, 6)
                nc.tensor.matmul(bank[0][0:LO, 0:HI], zeros[:, 0:LO], zeros[:, 0:HI], start=True, stop=False)
                with pe.Fori(0, STEPS) as it:
                    for j in range(GROUPS_PER_STEP):
                        pe.wait_ge(s_hot, (it * GROUPS_PER_STEP + j) * 2 + 2)
                        for c in range(GROUP):
                            last = nc.tensor.matmul(bank[0][0:LO, 0:HI], onehot_lo[:, j, c], onehot_hi[:, j, c],
                                                    start=False, stop=False)
                        last.then_inc(s_hot_used, 1)
                nc.tensor.matmul(bank[0][0:LO, 0:HI], zeros[:, 0:LO], zeros[:, 0:HI], start=False, stop=True)\
                    .then_inc(s_deg, 1)
                pe.wait_ge(s_wt, 160)
                pe.sem_inc(s_xt, BATCH)
                pe.sem_inc(s_rows, 2)
                with pe.Fori(0, PASSES) as it:
                    for j in range(BATCH):
                        t = it * BATCH + j
                        pe.wait_ge(s_xn, t + 1)
                        for k in range(HALF):
                            last = nc.tensor.transpose(bank[1 + j % 2][:, k * P:(k + 1) * P],
                                                       buf_a[:, j, k * P:(k + 1) * P], ident[:])
                        last.then_inc(s_xn_t, 1)
                        pe.wait_ge(s_xt, t + 1 + BATCH)
                        pe.wait_ge(s_rows, t + (2 if j == 0 else 1))
                        for k in range(HALF):
                            last = nc.tensor.matmul(bank[3 + j % 2][:, 0:D], buf_b[:, j, k * P:(k + 1) * P],
                                                    w1_sb[:, k, :], start=(k == 0), stop=(k == HALF - 1))
                        last.then_inc(s_h, 1)

        setup_ctx.close()
        agg = sb("agg", [P, HALF, AGG])
        place = sb("place", [P, GROUPS_PER_STEP, GROUP, WINDOW])
        sum_rows = sb("sum_rows", [WINDOW, D])
        buf_c = sb("buf_c", [P, BATCH, D])

        def write_table(tag, second):
            s_relu = sem(f"relu_{tag}")
            s_u = sem(f"product_{tag}")
            s_v = sem(f"biased_{tag}")
            s_g = sem(f"table_rows_{tag}")
            s_gt = sem(f"table_rows_transposed_{tag}")
            s_loops = sem(f"self_loops_{tag}")
            s_store = [sem(f"table_store_{tag}{j}") for j in range(BATCH)]
            s_stored = sem(f"table_stored_{tag}")

            with nc.Block() as block:
                @block.sync
                def _(sp):
                    sp.sem_inc(s_stored, 1)
                    with sp.Fori(0, PASSES) as it:
                        for j in range(BATCH):
                            t = it * BATCH + j
                            sp.wait_ge(s_g, t + 1)
                            sp.dma_start(table[bass.ds(t * P, P), :], buf_a[:, j, :]).then_inc(s_store[j], 16)
                        for j in range(BATCH):
                            sp.wait_ge(s_store[j], it * 16 + 16)
                        sp.sem_inc(s_stored, 1)

                @block.scalar
                def _(act):
                    with act.Fori(0, PASSES) as it:
                        if second:
                            for j in range(BATCH):
                                t = it * BATCH + j
                                nc.scalar.activation(buf_b[:, j, :].rearrange("p (k n) -> p k n", k=HALF),
                                                     agg[:, :, bass.ds(t * P, P)], ACT.Relu).then_inc(s_relu, 1)
                        act.wait_ge(s_stored, it + 1)
                        act.wait_ge(s_gt, it * BATCH + 1)
                        for j in range(BATCH):
                            t = it * BATCH + j
                            if second:
                                act.wait_ge(s_v, t + 1)
                                source = buf_c[:, j, :]
                            else:
                                source = rows[:, bass.ds(t, 1), :].rearrange("p a b -> p (a b)")
                            nc.scalar.activation(buf_a[:, j, :], source, ACT.Copy,
                                                 scale=dinv[:, bass.ds(t, 1)]).then_inc(s_g, 1)

                @block.vector
                def _(dve):
                    if not second:
                        nc.vector.memset(agg[:, :, NODES:AGG], 0.0)
                    with dve.Fori(0, PASSES) as it:
                        if second:
                            for j in range(BATCH):
                                t = it * BATCH + j
                                dve.wait_ge(s_u, t + 1)
                                nc.vector.scalar_tensor_tensor(buf_c[:, j, :], bank[3 + j % 2][:, 0:D],
                                                               dinv[:, bass.ds(t, 1)], b2_sb[:],
                                                               ALU.mult, ALU.add).then_inc(s_v, 1)
                        for j in range(BATCH):
                            t = it * BATCH + j
                            dve.wait_ge(s_gt, t + 2)
                            nc.vector.tensor_copy(agg[:, :, bass.ds(t * P, P)],
                                                  bank[1 + j % 2][:, 0:D].rearrange("p (k n) -> p k n", k=HALF))\
                                .then_inc(s_loops, 1)

                @block.tensor
                def _(pe):
                    pe.sem_inc(s_gt, 1)
                    pe.sem_inc(s_loops, 2)
                    with pe.Fori(0, PASSES) as it:
                        if second:
                            for j in range(BATCH):
                                t = it * BATCH + j
                                pe.wait_ge(s_relu, t + 1)
                                if j >= 2:
                                    pe.wait_ge(s_v, t - 1)
                                for k in range(HALF):
                                    last = nc.tensor.matmul(bank[3 + j % 2][:, 0:D],
                                                            buf_b[:, j, k * P:(k + 1) * P], w2_sb[:, k, :],
                                                            start=(k == 0), stop=(k == HALF - 1))
                                last.then_inc(s_u, 1)
                        for j in range(BATCH):
                            t = it * BATCH + j
                            pe.wait_ge(s_g, t + 1)
                            pe.wait_ge(s_loops, t + (2 if j == 0 else 1))
                            for k in range(HALF):
                                last = nc.tensor.transpose(bank[1 + j % 2][:, k * P:(k + 1) * P],
                                                           buf_a[:, j, k * P:(k + 1) * P], ident[:])
                            last.then_inc(s_gt, 1)

        def sum_edges(tag, rounds):
            s_start = sem(f"windows_{tag}")
            s_idx = [sem(f"indices_{tag}{j}") for j in range(GROUPS_PER_STEP)]
            s_row = [sem(f"rows_gathered_{tag}{j}") for j in range(GROUPS_PER_STEP)]
            s_eq = sem(f"edge_columns_{tag}")
            s_place = sem(f"placed_{tag}")
            s_sum = sem(f"group_summed_{tag}")
            s_copy = sem(f"sums_copied_{tag}")
            s_t = sem(f"sums_transposed_{tag}")
            s_add = sem(f"sums_added_{tag}")
            s_next = sem(f"next_round_{tag}")
            s_turn = sem(f"turn_{tag}")

            with nc.Block() as block:
                @block.vector
                def _(dve):
                    nc.vector.tensor_copy(base_i[:], base_f[:]).then_inc(s_start, 1)
                    nc.vector.tensor_tensor(dst_rel[:].rearrange("p (g c) -> p g c", c=GROUP),
                                            dst_f[:].rearrange("p (g c) -> p g c", c=GROUP),
                                            base_f[:].unsqueeze(2).to_broadcast([P, GROUPS + 1, GROUP]),
                                            ALU.subtract).then_inc(s_start, 1)
                    dve.wait_ge(s_start, 2)
                    dve.sem_inc(s_add, 1)

                @block.tensor
                def _(pe):
                    pe.sem_inc(s_sum, GROUPS_PER_STEP)

            with nc.Fori(0, rounds) as rnd:
                with nc.Block() as block:
                    def group(it, j):
                        return (rnd * STEPS + it) * GROUPS_PER_STEP + j

                    @block.sync
                    def _(sp):
                        with sp.Fori(0, STEPS) as it:
                            for j in range(GROUPS_PER_STEP):
                                sp.wait_ge(s_sum, group(it, j) + 1)
                                sp.dma_start(idx[:, j, :], src[:, bass.ds(it * CHUNKS_PER_STEP + j * GROUP, GROUP)])\
                                    .then_inc(s_idx[j], 16)

                    @block.gpsimd
                    def _(pool):
                        with pool.Fori(0, STEPS) as it:
                            for j in range(GROUPS_PER_STEP):
                                pool.wait_ge(s_idx[j], (rnd * STEPS + it) * 16 + 16)
                                pool.sem_inc(s_turn, 1)
                                for c in range(GROUP):
                                    nc.gpsimd.indirect_dma_start(
                                        ring[:, j * GROUP + c, :], None, table,
                                        bass.IndirectOffsetOnAxis(ap=idx[:, j, c:c + 1], axis=0))\
                                        .then_inc(s_row[j], 16)

                    @block.vector
                    def _(dve):
                        def build(it, j, n):
                            c = it * CHUNKS_PER_STEP + j * GROUP
                            slot = j % GROUPS_PER_STEP
                            dve.wait_ge(s_sum, n + 1)
                            nc.vector.tensor_tensor(
                                place[:, slot], bc(iota[:, 0:WINDOW].unsqueeze(1), [P, GROUP, WINDOW]),
                                bc(dst_rel[:, bass.ds(c, GROUP)].unsqueeze(2), [P, GROUP, WINDOW]),
                                ALU.is_equal).then_inc(s_eq, 1)
                            return c, slot

                        def weigh(c, slot, n):
                            dve.wait_ge(s_eq, n + 1)
                            nc.vector.tensor_tensor(
                                place[:, slot], place[:, slot],
                                bc(w_edge[:, bass.ds(c, GROUP)].unsqueeze(2), [P, GROUP, WINDOW]),
                                ALU.mult).then_inc(s_place, 1)

                        with dve.Fori(0, STEPS) as it:
                            for j in range(GROUPS_PER_STEP):
                                n = group(it, j)
                                c, slot = build(it, j, n)
                                first = dve.value_load(base_i[0:1, bass.ds(it * GROUPS_PER_STEP + j, 1)],
                                                       min_val=0, max_val=NODES)
                                weigh(c, slot, n)
                                dve.wait_ge(s_t, n + 1)
                                dve.wait_ge(s_add, n + 1)
                                window = agg[:, :, bass.ds(first, WINDOW)]
                                nc.vector.tensor_tensor(window, window, bank[1][:, 0:HALF * WINDOW]
                                                        .rearrange("p (k n) -> p k n", k=HALF),
                                                        ALU.add).then_inc(s_add, 1)
                        nc.vector.tensor_scalar(base_i[:], base_i[:], float(WINDOW), float(NODES), ALU.add,
                                                ALU.min).then_inc(s_next, 1)
                        nc.vector.tensor_scalar(dst_rel[:], dst_rel[:], -float(WINDOW), None, ALU.add)\
                            .then_inc(s_next, 1)
                        dve.wait_ge(s_next, rnd * 2 + 2)
                        dve.sem_inc(s_turn, 1)

                    @block.scalar
                    def _(act):
                        with act.Fori(0, STEPS) as it:
                            for j in range(GROUPS_PER_STEP):
                                act.wait_ge(s_sum, group(it, j) + 1 + GROUPS_PER_STEP)
                                nc.scalar.activation(sum_rows[:], bank[0][0:WINDOW, 0:D], ACT.Copy).then_inc(s_copy, 1)

                    @block.tensor
                    def _(pe):
                        with pe.Fori(0, STEPS) as it:
                            for j in range(GROUPS_PER_STEP):
                                n = group(it, j)
                                pe.wait_ge(s_place, n + 1)
                                pe.wait_ge(s_row[j], (rnd * STEPS + it) * (16 * GROUP) + 16 * GROUP)
                                for c in range(GROUP):
                                    last = nc.tensor.matmul(bank[0][0:WINDOW, 0:D], place[:, j, c],
                                                            ring[:, j * GROUP + c, :],
                                                            start=(c == 0), stop=(c == GROUP - 1))
                                last.then_inc(s_sum, 1)
                                pe.wait_ge(s_copy, n + 1)
                                pe.wait_ge(s_add, n + 1)
                                pe.sem_inc(s_turn, 1)
                                for k in range(HALF):
                                    last = nc.tensor.transpose(bank[1][:, k * WINDOW:(k + 1) * WINDOW],
                                                               sum_rows[:, k * P:(k + 1) * P],
                                                               ident[0:WINDOW, 0:WINDOW])
                                last.then_inc(s_t, 1)

        def experts():
            x_in = buf_a[:, 0, :]
            x1 = buf_a[:, 1, :]
            y = buf_a[:, 2, :]
            x1_y = buf_a[:, 3, :]
            y_t = buf_a[:, 4, :]
            total = buf_a[:, 5, :]
            relu_t = buf_a[:, 6, :]
            hidden = [buf_b[:, i, :] for i in range(2)]
            small = sb("small", [P, 64])
            mstat, mv = small[:, 0:6], small[:, 6:8]
            inv_std, neg_mean = small[:, 8:9], small[:, 9:10]
            neg_max, exp_sum, exp_inv = small[:, 10:11], small[:, 11:12], small[:, 12:13]
            pair_sum, pair_inv = small[:, 13:14], small[:, 14:15]
            top_w = small[:, 16:18]
            top_i = small[:, 18:26]
            prob = small[:, 26:34]
            top_p = small[:, 34:42]
            comb_0, comb_1, comb = small[:, 42:50], small[:, 50:58], sb("comb", [P, EXPERTS])
            top_u = sb("top_u", [P, 8], mybir.dt.uint32)
            comb_t = sb("comb_t", [EXPERTS, P])
            rows_p, y_t_p = bank[2][:, 0:D], bank[2][:, D:2 * D]
            logits_p, comb_t_p, bias_p = bank[3][:, 0:EXPERTS], bank[3][0:EXPERTS, P:2 * P], bank[3][:, D:2 * D]
            hidden_p = [bank[4][:, 0:D], bank[5][:, 0:D]]
            expert_p = [bank[6][:, 0:D], bank[7][:, 0:D]]

            s_x = sem("tile_loaded")
            s_relu = sem("tile_relu")
            s_rows = sem("tile_rows")
            s_x1 = sem("tile_residual")
            s_var = sem("tile_variance")
            s_std = sem("tile_deviation")
            s_y = sem("tile_normalised")
            s_yt = sem("tile_transposed")
            s_yt_sb = sem("tile_transposed_copied")
            s_logit = sem("logits")
            s_nmax = sem("logit_max")
            s_exp = sem("logit_exp")
            s_comb = sem("combine_ready")
            s_comb_t = sem("combine_transposed")
            s_comb_sb = sem("combine_copied")
            s_bias = sem("combined_bias")
            s_hid = sem("hidden_product")
            s_gelu = sem("hidden_ready")
            s_exp_y = sem("expert_product")
            s_acc = sem("expert_added")
            s_store = sem("tile_store")
            s_free = sem("total_free")
            s_chain = sem("expert_vector_step")

            with nc.Block() as block:
                @block.sync
                def _(sp):
                    def load(m, first):
                        if not first:
                            sp.wait_ge(s_x1, m)
                        sp.dma_start(x_in, x[bass.ds(m * P, P), :]).then_inc(s_x, 16)
                    load(0, True)
                    sp.sem_inc(s_free, 1)
                    with sp.Fori(0, TILES) as t:
                        load(t + 1, False)
                        sp.wait_ge(s_acc, (t + 1) * EXPERTS + 2)
                        sp.dma_start(out[bass.ds(t * P, P), :], total).then_inc(s_store, 16)
                        sp.wait_ge(s_store, t * 16 + 16)
                        sp.sem_inc(s_free, 1)

                @block.scalar
                def _(act):
                    def prepare_relu(m, first):
                        if not first:
                            act.wait_ge(s_rows, m)
                        nc.scalar.activation(relu_t.rearrange("p (k n) -> p k n", k=HALF),
                                             agg[:, :, bass.ds(m * P, P)], ACT.Relu).then_inc(s_relu, 1)

                    def prepare_std(m):
                        act.wait_ge(s_var, m + 1)
                        nc.scalar.activation(inv_std, mv[:, 1:2], ACT.Sqrt, bias=eps[:, 0:1]).then_inc(s_std, 1)

                    def gelu(t, e):
                        act.wait_ge(s_hid, t * EXPERTS + e + 2)
                        act.wait_ge(s_exp_y, t * EXPERTS + e + 1)
                        for k in range(HALF):
                            nc.scalar.activation(hidden[e % 2][:, k * P:(k + 1) * P],
                                                 hidden_p[e % 2][:, k * P:(k + 1) * P], ACT.Gelu,
                                                 bias=moe_b1_sb[:, e * HALF + k:e * HALF + k + 1])\
                                .then_inc(s_gelu, 1)

                    prepare_relu(0, True)
                    prepare_std(0)
                    with act.Fori(0, TILES) as t:
                        act.wait_ge(s_yt, t + 1)
                        act.wait_ge(s_hid, t * EXPERTS + 1)
                        nc.scalar.activation(y_t, y_t_p, ACT.Copy).then_inc(s_yt_sb, 1)
                        act.wait_ge(s_nmax, t + 1)
                        nc.scalar.activation(prob, logits_p, ACT.Exp, bias=neg_max, accum_out=exp_sum)\
                            .then_inc(s_exp, 1)
                        prepare_relu(t + 1, False)
                        gelu(t, 0)
                        gelu(t, 1)
                        act.wait_ge(s_comb_t, t + 1)
                        nc.scalar.activation(comb_t[:], comb_t_p, ACT.Copy).then_inc(s_comb_sb, 1)
                        gelu(t, 2)
                        gelu(t, 3)
                        gelu(t, 4)
                        prepare_std(t + 1)
                        gelu(t, 5)
                        gelu(t, 6)
                        gelu(t, 7)

                @block.vector
                def _(dve):
                    chain = [0]

                    def step(ins):
                        chain[0] += 1
                        ins.then_inc(s_chain, 1)
                        dve.wait_ge(s_chain, chain[0])

                    def prepare(m, first):
                        dve.wait_ge(s_rows, m + 1)
                        dve.wait_ge(s_x, m * 16 + 16)
                        nc.vector.scalar_tensor_tensor(x1, rows_p, dinv[:, bass.ds(m, 1)], x_in, ALU.mult,
                                                       ALU.add).then_inc(s_x1, 1)
                        dve.wait_ge(s_x1, m + 1)
                        step(nc.vector.bn_stats(mstat, x1))
                        nc.vector.bn_aggr(mv, mstat).then_inc(s_var, 1)
                        dve.wait_ge(s_std, m + 1)
                        step(nc.vector.reciprocal(inv_std, inv_std))
                        step(nc.vector.scalar_tensor_tensor(neg_mean, mv[:, 0:1], -1.0, inv_std, ALU.mult, ALU.mult))
                        if not first:
                            dve.wait_ge(s_yt, m)
                        nc.vector.tensor_scalar(y, x1, inv_std, neg_mean, ALU.mult, ALU.add).then_inc(s_y, 1)
                        dve.wait_ge(s_y, m + 1)
                        step(nc.vector.tensor_tensor(x1_y, x1, y, ALU.add))

                    def add_expert(t, e):
                        dve.wait_ge(s_exp_y, t * EXPERTS + e + 3)
                        dve.wait_ge(s_acc, t * EXPERTS + e + 2)
                        nc.vector.scalar_tensor_tensor(total, expert_p[e % 2], comb[:, e:e + 1], total,
                                                       ALU.mult, ALU.add).then_inc(s_acc, 1)

                    prepare(0, True)
                    with dve.Fori(0, TILES) as t:
                        dve.sem_clear(s_chain)
                        chain[0] = 0
                        dve.wait_ge(s_logit, t + 1)
                        nc.vector.tensor_reduce(neg_max, logits_p, AX, ALU.max, negate=True).then_inc(s_nmax, 1)
                        dve.wait_ge(s_exp, t + 1)
                        step(nc.vector.reciprocal(exp_inv, exp_sum))
                        step(nc.vector.tensor_scalar(prob, prob, exp_inv, None, ALU.mult))
                        step(nc.vector.max(top_p, prob))
                        step(nc.vector.max_index(top_u[:], top_p, prob))
                        step(nc.vector.tensor_copy(top_i, top_u[:]))
                        step(nc.vector.tensor_tensor(pair_sum, top_p[:, 0:1], top_p[:, 1:2], ALU.add))
                        step(nc.vector.tensor_scalar(pair_sum, pair_sum, 1e-12, None, ALU.max))
                        step(nc.vector.reciprocal(pair_inv, pair_sum))
                        step(nc.vector.tensor_scalar(top_w, top_p[:, 0:2], pair_inv, None, ALU.mult))
                        step(nc.vector.tensor_scalar(comb_0, iota[:, 0:EXPERTS], top_i[:, 0:1], top_w[:, 0:1],
                                                     ALU.is_equal, ALU.mult))
                        step(nc.vector.tensor_scalar(comb_1, iota[:, 0:EXPERTS], top_i[:, 1:2], top_w[:, 1:2],
                                                     ALU.is_equal, ALU.mult))
                        nc.vector.tensor_tensor(comb[:], comb_0, comb_1, ALU.add).then_inc(s_comb, 1)
                        dve.wait_ge(s_bias, t + 1)
                        dve.wait_ge(s_free, t + 1)
                        step(nc.vector.tensor_tensor(total, bias_p, x1_y, ALU.add))
                        for e in range(5):
                            add_expert(t, e)
                            if e == 1:
                                prepare(t + 1, False)
                        for e in range(5, EXPERTS):
                            add_expert(t, e)

                @block.tensor
                def _(pe):
                    pe.sem_inc(s_hid, 1)
                    pe.sem_inc(s_exp_y, 2)
                    pe.sem_inc(s_acc, 2)

                    def prepare_rows(m):
                        pe.wait_ge(s_relu, m + 1)
                        for k in range(HALF):
                            last = nc.tensor.transpose(rows_p[:, k * P:(k + 1) * P], relu_t[:, k * P:(k + 1) * P],
                                                       ident[:])
                        last.then_inc(s_rows, 1)

                    def prepare_y(m, first):
                        pe.wait_ge(s_y, m + 1)
                        if not first:
                            pe.wait_ge(s_yt_sb, m)
                        for k in range(HALF):
                            last = nc.tensor.transpose(y_t_p[:, k * P:(k + 1) * P], y[:, k * P:(k + 1) * P], ident[:])
                        last.then_inc(s_yt, 1)

                    def hidden_product(e):
                        for f in range(HALF):
                            for k in range(HALF):
                                last = nc.tensor.matmul(hidden_p[e % 2][:, f * P:(f + 1) * P],
                                                        moe_w1_sb[:, e, k, f * P:(f + 1) * P],
                                                        y_t[:, k * P:(k + 1) * P], start=(k == 0), stop=(k == 1))
                        last.then_inc(s_hid, 1)

                    def expert_product(t, e):
                        pe.wait_ge(s_gelu, (t * EXPERTS + e) * HALF + HALF)
                        pe.wait_ge(s_acc, t * EXPERTS + e + 1)
                        for f in range(HALF):
                            last = nc.tensor.matmul(expert_p[e % 2], hidden[e % 2][:, f * P:(f + 1) * P],
                                                    moe_w2_sb[:, e, f, :], start=(f == 0), stop=(f == 1))
                        last.then_inc(s_exp_y, 1)

                    prepare_rows(0)
                    prepare_y(0, True)
                    with pe.Fori(0, TILES) as t:
                        pe.wait_ge(s_yt_sb, t + 1)
                        for k in range(HALF):
                            last = nc.tensor.matmul(logits_p, y_t[:, k * P:(k + 1) * P], router_sb[:, k, :],
                                                    start=(k == 0), stop=(k == 1))
                        last.then_inc(s_logit, 1)
                        hidden_product(0)
                        hidden_product(1)
                        prepare_rows(t + 1)
                        pe.wait_ge(s_comb, t + 1)
                        nc.tensor.transpose(comb_t_p, comb[:], ident[:]).then_inc(s_comb_t, 1)
                        expert_product(t, 0)
                        pe.wait_ge(s_comb_sb, t + 1)
                        nc.tensor.matmul(bias_p, comb_t[:], moe_b2_sb[:], start=True, stop=True).then_inc(s_bias, 1)
                        for e in range(2, EXPERTS):
                            hidden_product(e)
                            expert_product(t, e - 1)
                            if e == 6:
                                prepare_y(t + 1, False)
                        expert_product(t, EXPERTS - 1)

        write_table("l1", second=False)
        rounds = nc.values_load(rounds_i[0:1, 0:1], min_val=1, max_val=NODES // WINDOW + 1)
        sum_edges("l1", rounds)
        write_table("l2", second=True)
        sum_edges("l2", rounds)
        experts()


def kernel(x, src, dst, edge_weight1, L0_gnn_W1, L0_gnn_b1, L0_gnn_W2, L0_gnn_b2,
           L0_ffn_router_w, L0_ffn_w1, L0_ffn_b1, L0_ffn_w2, L0_ffn_b2):
    import numpy as np
    import concourse.bacc as bacc
    from concourse.bass_utils import run_bass_kernel_spmd

    def by_partition(edges, fill):
        flat = np.full(CHUNKS_PAD * P, fill, edges.dtype)
        flat[:N_EDGES] = edges
        return flat.reshape(CHUNKS_PAD, P).T

    x = np.asarray(x)
    x_pad = np.zeros((TILES_PAD * P, D), x.dtype)
    x_pad[:N_NODES] = x
    b1 = np.asarray(L0_ffn_b1).reshape(EXPERTS * HALF, P).T
    ins = {
        "x": x_pad,
        "src": by_partition(np.asarray(src), 0),
        "dst": by_partition(np.asarray(dst), N_NODES),
        "weight": by_partition(np.asarray(edge_weight1)[:, 0], 0),
        "gnn_w1": np.asarray(L0_gnn_W1).T, "gnn_b1": np.asarray(L0_gnn_b1),
        "gnn_w2": np.asarray(L0_gnn_W2).T, "gnn_b2": np.asarray(L0_gnn_b2),
        "router": np.asarray(L0_ffn_router_w).T,
        "moe_w1": np.asarray(L0_ffn_w1), "moe_b1": b1,
        "moe_w2": np.asarray(L0_ffn_w2), "moe_b2": np.asarray(L0_ffn_b2),
    }
    ins = {f"in_{n}": np.ascontiguousarray(a) for n, a in ins.items()}
    nc = bacc.Bacc("TRN2", target_bir_lowering=False, num_devices=1)
    args = [nc.dram_tensor(n, a.shape, mybir.dt.from_np(a.dtype), kind="ExternalInput").ap() for n, a in ins.items()]
    out = nc.dram_tensor("out_rows", (NODES, D), F32, kind="ExternalOutput").ap()
    gnn_ffn_kernel(nc, *args, out)
    r = run_bass_kernel_spmd(nc, [ins], core_ids=[0])
    return r.results[0]["out_rows"][:N_NODES]
```

```python
import concourse.bass as bass
from concourse import mybir
from contextlib import ExitStack

F32 = mybir.dt.float32
BF16 = mybir.dt.bfloat16
I32 = mybir.dt.int32
ALU = mybir.AluOpType
ACT = mybir.ActivationFunctionType
AX = mybir.AxisListType.X

P = 128
D = 256
HALF = D // P
N_NODES = 6250
N_EDGES = 206250
EXPERTS = 8
TILES = -(-N_NODES // P)
NODES = TILES * P
TILES_PAD = TILES + 1
GROUP = 11
GROUPS_PER_STEP = 3
STEPS = TILES
CHUNKS_PER_STEP = GROUP * GROUPS_PER_STEP
CHUNKS = STEPS * CHUNKS_PER_STEP
GROUPS = STEPS * GROUPS_PER_STEP
CHUNKS_PAD = CHUNKS + GROUP
assert CHUNKS * P >= N_EDGES
WINDOW = 64
AGG = TILES_PAD * P
LO = 64
HI = NODES // LO
BATCH = 7
PASSES = TILES // BATCH
assert BATCH * PASSES == TILES and HI * LO == NODES and HI == 2 * TILES
EPS = 1e-5
RMAX = bass.bass_isa.ReduceOp.max


class Parts:
    pass


def gnn_ffn_kernel(nc, x, src, dst, weight, gnn_w1, gnn_b1, gnn_w2, gnn_b2,
                   router, moe_w1, moe_b1, moe_w2, moe_b2, out):
    ctx = ExitStack()
    with ctx:
        def sb(name, shape, dt=F32):
            return ctx.enter_context(nc.sbuf_tensor(name, shape, dt))

        def sem(name):
            return ctx.enter_context(nc.semaphore(name))

        table_1 = nc.dram_tensor("table_1", [NODES, D], F32, kind="Internal").ap()
        table_2 = nc.dram_tensor("table_2", [NODES, D], F32, kind="Internal").ap()
        x_tiles = x.rearrange("(t p) d -> p t d", p=P)

        rows = sb("rows", [P, TILES, D])
        ring = rows[:, 0:CHUNKS_PER_STEP, :]
        dst_f = sb("dst_f", [P, CHUNKS_PAD])
        dst_rel = sb("dst_rel", [P, CHUNKS_PAD])
        w_edge = sb("w_edge", [P, CHUNKS_PAD])
        idx = sb("idx", [P, GROUPS_PER_STEP, GROUP], I32)
        base_f = sb("base_f", [P, GROUPS + 1])
        base_i = sb("base_i", [P, GROUPS + 1], I32)
        choice_i = sb("choice_i", [P, 2], I32)
        iota = sb("iota", [P, P])
        ident = sb("ident", [P, P])
        w1_sb = sb("w1_sb", [P, HALF, D])
        w2_sb = sb("w2_sb", [P, HALF, D])
        b1_sb = sb("b1_sb", [P, D])
        b2_sb = sb("b2_sb", [P, D])
        router_sb = sb("router_sb", [P, HALF, EXPERTS])
        moe_w1_sb = sb("moe_w1_sb", [P, EXPERTS, HALF, D])
        moe_w2_sb = sb("moe_w2_sb", [P, EXPERTS, HALF, D])
        moe_b1_sb = sb("moe_b1_sb", [P, EXPERTS * HALF])
        moe_b2_sb = sb("moe_b2_sb", [EXPERTS, D])
        eps = sb("eps", [P, 1])
        dinv = sb("dinv", [P, TILES_PAD])
        buf_a = sb("buf_a", [P, BATCH, D])
        buf_b = sb("buf_b", [P, BATCH, D])

        bank = [ctx.enter_context(nc.psum_tensor(f"bank{i}", [P, 512], F32)) for i in range(8)]

        bc = lambda ap, shape: ap.to_broadcast(shape)

        setup_ctx = ExitStack()

        def tmp(name, shape, dt=F32):
            return setup_ctx.enter_context(nc.sbuf_tensor(name, shape, dt))

        dst_i = tmp("dst_i", [P, CHUNKS_PAD], I32)
        lo_i = tmp("lo_i", [P, CHUNKS_PAD], I32)
        lo_b = tmp("lo_b", [P, CHUNKS_PAD], BF16)
        hi_b = tmp("hi_b", [P, CHUNKS_PAD], BF16)
        onehot_lo = tmp("onehot_lo", [P, GROUPS_PER_STEP, GROUP, LO], BF16)
        onehot_hi = tmp("onehot_hi", [P, GROUPS_PER_STEP, GROUP, HI], BF16)
        extent = tmp("extent", [P, 2, GROUPS + 1])
        extent_all = tmp("extent_all", [P, 2, GROUPS + 1])
        span = tmp("span", [P, GROUPS + 1])
        span_max = tmp("span_max", [P, 1])
        span_i = tmp("span_i", [P, 1], I32)
        slack = tmp("slack", [P, 1])
        tile_due = tmp("tile_due", [P, GROUPS + 3])
        iota_lo = tmp("iota_lo", [P, LO], BF16)
        iota_hi = tmp("iota_hi", [P, HI], BF16)
        zeros = tmp("zeros", [P, P], BF16)
        deg_lohi = tmp("deg_lohi", [LO, TILES, 2])
        deg = tmp("deg", [P, TILES])
        deg_root = tmp("deg_root", [P, TILES])
        stats = tmp("stats", [P, TILES, 6])
        mean = tmp("mean", [P, TILES])
        var = tmp("var", [P, TILES])
        gap = tmp("gap", [P, TILES])
        rstd = tmp("rstd", [P, TILES])
        shift = tmp("shift", [P, TILES])

        s_edge = sem("edges_loaded")
        s_wt = sem("weights_loaded")
        s_x = [sem(f"x_loaded{i}") for i in range(PASSES)]
        s_const = sem("constants_ready")
        s_split = sem("dst_split")
        s_extent = sem("extent_ready")
        s_extent_all = sem("extent_reduced")
        s_hot = sem("onehots_ready")
        s_hot_used = sem("onehots_used")
        s_deg = sem("degree_counted")
        s_deg_sb = sem("degree_copied")
        s_deg_tile = sem("degree_by_tile")
        s_root = sem("degree_root")
        s_dinv = sem("dinv_ready")
        s_var = sem("variance_ready")
        s_std = sem("deviation_ready")
        s_norm = sem("norm_factors_ready")
        s_xn = sem("normalised_rows")
        s_xn_t = sem("rows_transposed")
        s_xt = sem("transposed_copied")
        s_h = sem("h_matmul")
        s_rows = sem("h_rows_ready")
        s_chain_v = sem("vector_step")
        s_chain_g = sem("gpsimd_step")

        with nc.Block() as block:
            @block.sync
            def _(sp):
                sp.dma_start(dst_i[:], dst).then_inc(s_edge, 16)
                for i in range(PASSES):
                    t = slice(i * BATCH, (i + 1) * BATCH)
                    sp.dma_start(rows[:, t, :], x_tiles[:, t, :]).then_inc(s_x[i], 16)
                sp.dma_start(w_edge[:], weight).then_inc(s_wt, 16)
                sp.wait_ge(s_deg_sb, 1)
                for odd in range(2):
                    with nc.allow_non_contiguous_dma(reason="49 degrees per partition"):
                        sp.dma_start(deg[odd * LO:(odd + 1) * LO, :], deg_lohi[:, :, odd]).then_inc(s_deg_tile, 16)
                sp.wait_ge(s_wt, 16)

            @block.scalar
            def _(act):
                act.dma_start(w1_sb[:], gnn_w1.rearrange("(k p) n -> p k n", p=P)).then_inc(s_wt, 16)
                act.dma_start(b1_sb[:], gnn_b1.partition_broadcast(P)).then_inc(s_wt, 16)
                act.dma_start(w2_sb[:], gnn_w2.rearrange("(k p) n -> p k n", p=P)).then_inc(s_wt, 16)
                act.dma_start(b2_sb[:], gnn_b2.partition_broadcast(P)).then_inc(s_wt, 16)
                act.dma_start(router_sb[:], router.rearrange("(k p) n -> p k n", p=P)).then_inc(s_wt, 16)
                act.dma_start(moe_w1_sb[:], moe_w1.rearrange("e (k p) n -> p e k n", p=P)).then_inc(s_wt, 16)
                act.dma_start(moe_w2_sb[:], moe_w2.rearrange("e (k p) n -> p e k n", p=P)).then_inc(s_wt, 16)
                act.dma_start(moe_b1_sb[:], moe_b1).then_inc(s_wt, 16)
                act.dma_start(moe_b2_sb[:], moe_b2).then_inc(s_wt, 16)
                act.wait_ge(s_const, 7)
                act.wait_ge(s_var, 1)
                nc.scalar.activation(rstd[:], var[:], ACT.Sqrt, bias=eps[:, 0:1]).then_inc(s_std, 1)
                act.wait_ge(s_norm, 1)
                with act.Fori(0, PASSES) as it:
                    for j in range(BATCH):
                        t = it * BATCH + j
                        act.wait_ge(s_xt, t + 1)
                        nc.scalar.activation(buf_a[:, j, :], rows[:, bass.ds(t, 1), :], ACT.Identity,
                                             scale=rstd[:, bass.ds(t, 1)],
                                             bias=shift[:, bass.ds(t, 1)]).then_inc(s_xn, 1)
                act.wait_ge(s_deg_tile, 32)
                nc.scalar.activation(deg_root[:], deg[:], ACT.Sqrt, bias=1.0).then_inc(s_root, 1)

            @block.gpsimd
            def _(pool):
                def step(ins, n):
                    ins.then_inc(s_chain_g, 1)
                    pool.wait_ge(s_chain_g, n)
                nc.gpsimd.iota(iota[:], pattern=[[1, P]], base=0, channel_multiplier=0,
                               allow_small_or_imprecise_dtypes=True).then_inc(s_const, 1)
                nc.gpsimd.iota(iota_lo[:], pattern=[[1, LO]], base=0, channel_multiplier=0,
                               allow_small_or_imprecise_dtypes=True).then_inc(s_const, 1)
                nc.gpsimd.iota(iota_hi[:], pattern=[[1, HI]], base=0, channel_multiplier=0,
                               allow_small_or_imprecise_dtypes=True).then_inc(s_const, 1)
                nc.gpsimd.iota(tile_due[:], pattern=[[P, STEPS + 1], [0, GROUPS_PER_STEP]], base=-P,
                               channel_multiplier=0, allow_small_or_imprecise_dtypes=True).then_inc(s_const, 1)
                nc.gpsimd.memset(zeros[:], 0.0).then_inc(s_const, 1)
                nc.gpsimd.memset(eps[:], EPS).then_inc(s_const, 1)
                step(nc.gpsimd.memset(ident[:], 0.0), 1)
                nc.gpsimd.affine_select(out=ident[:], in_=ident[:], compare_op=ALU.not_equal, fill=1.0,
                                        base=0, pattern=[[-1, P]], channel_multiplier=1).then_inc(s_const, 1)
                pool.wait_ge(s_extent, 2)
                nc.gpsimd.partition_all_reduce(extent_all[:].rearrange("p a g -> p (a g)"),
                                               extent[:].rearrange("p a g -> p (a g)"), P, RMAX)\
                    .then_inc(s_extent_all, 1)

            @block.vector
            def _(dve):
                chain = [0]

                def step(ins):
                    chain[0] += 1
                    ins.then_inc(s_chain_v, 1)
                    dve.wait_ge(s_chain_v, chain[0])

                def norm_stats():
                    for i in range(PASSES):
                        dve.wait_ge(s_x[i], 16)
                    with dve.Fori(0, TILES) as t:
                        nc.vector.bn_stats(stats[:, bass.ds(t, 1), :].rearrange("p a b -> p (a b)"),
                                           rows[:, bass.ds(t, 1), :].rearrange("p a b -> p (a b)"))\
                            .then_inc(s_chain_v, 1)
                    chain[0] += TILES
                    dve.wait_ge(s_chain_v, chain[0])
                    st = lambda k: stats[:, :, k]
                    nc.vector.tensor_tensor(mean[:], st(1), st(4), ALU.add).then_inc(s_chain_v, 1)
                    nc.vector.tensor_tensor(gap[:], st(1), st(4), ALU.subtract).then_inc(s_chain_v, 1)
                    nc.vector.tensor_tensor(var[:], st(2), st(5), ALU.add).then_inc(s_chain_v, 1)
                    chain[0] += 3
                    dve.wait_ge(s_chain_v, chain[0])
                    step(nc.vector.tensor_tensor(gap[:], gap[:], gap[:], ALU.mult))
                    nc.vector.tensor_scalar(mean[:], mean[:], 0.5, None, ALU.mult).then_inc(s_chain_v, 1)
                    nc.vector.tensor_scalar(var[:], var[:], 1.0 / D, None, ALU.mult).then_inc(s_chain_v, 1)
                    chain[0] += 2
                    dve.wait_ge(s_chain_v, chain[0])
                    nc.vector.scalar_tensor_tensor(var[:], gap[:], 0.25, var[:], ALU.mult, ALU.add).then_inc(s_var, 1)
                    dve.wait_ge(s_std, 1)
                    step(nc.vector.reciprocal(rstd[:], rstd[:]))
                    nc.vector.scalar_tensor_tensor(shift[:], mean[:], -1.0, rstd[:], ALU.mult, ALU.mult)\
                        .then_inc(s_norm, 1)

                dve.wait_ge(s_edge, 16)
                nc.vector.tensor_copy(dst_f[:], dst_i[:]).then_inc(s_chain_v, 1)
                nc.vector.tensor_scalar(lo_i[:], dst_i[:], LO - 1, None, ALU.bitwise_and).then_inc(s_chain_v, 1)
                chain[0] += 2
                dve.wait_ge(s_chain_v, chain[0])
                step(nc.vector.tensor_copy(lo_b[:], lo_i[:]))
                step(nc.vector.tensor_scalar(lo_i[:], dst_i[:], LO.bit_length() - 1, None, ALU.logical_shift_right))
                nc.vector.tensor_copy(hi_b[:], lo_i[:]).then_inc(s_split, 1)
                by_group = dst_f[:].rearrange("p (g c) -> p g c", c=GROUP)
                nc.vector.tensor_reduce(extent[:, 0, :], by_group, AX, ALU.min, negate=True).then_inc(s_extent, 1)
                nc.vector.tensor_reduce(extent[:, 1, :], by_group, AX, ALU.max).then_inc(s_extent, 1)
                norm_stats()

                dve.wait_ge(s_const, 7)
                dve.wait_ge(s_split, 1)
                with dve.Fori(0, STEPS) as it:
                    for j in range(GROUPS_PER_STEP):
                        g = it * GROUPS_PER_STEP + j
                        dve.wait_ge(s_hot_used, g + 1)
                        c = it * CHUNKS_PER_STEP + j * GROUP
                        nc.vector.tensor_tensor(
                            onehot_lo[:, j], bc(iota_lo[:].unsqueeze(1), [P, GROUP, LO]),
                            bc(lo_b[:, bass.ds(c, GROUP)].unsqueeze(2), [P, GROUP, LO]), ALU.is_equal)\
                            .then_inc(s_hot, 1)
                        nc.vector.tensor_tensor(
                            onehot_hi[:, j], bc(iota_hi[:].unsqueeze(1), [P, GROUP, HI]),
                            bc(hi_b[:, bass.ds(c, GROUP)].unsqueeze(2), [P, GROUP, HI]), ALU.is_equal)\
                            .then_inc(s_hot, 1)

                dve.wait_ge(s_wt, 160)
                with dve.Fori(0, PASSES) as it:
                    for j in range(BATCH):
                        t = it * BATCH + j
                        dve.wait_ge(s_xn_t, t + 1)
                        nc.vector.tensor_copy(buf_b[:, j, :], bank[1 + j % 2][:, 0:D]).then_inc(s_xt, 1)
                        dve.wait_ge(s_h, t + 1)
                        nc.vector.tensor_tensor(rows[:, bass.ds(t, 1), :].rearrange("p a b -> p (a b)"),
                                                bank[3 + j % 2][:, 0:D], b1_sb[:], ALU.add).then_inc(s_rows, 1)

                dve.wait_ge(s_deg, 1)
                nc.vector.tensor_copy(deg_lohi[:], bank[0][0:LO, 0:HI].rearrange("p (t o) -> p t o", o=2))\
                    .then_inc(s_deg_sb, 1)
                dve.wait_ge(s_root, 1)
                nc.vector.memset(dinv[:, TILES:TILES_PAD], 1.0).then_inc(s_dinv, 1)
                nc.vector.reciprocal(dinv[:, 0:TILES], deg_root[:]).then_inc(s_dinv, 1)

                dve.wait_ge(s_extent_all, 1)
                nc.vector.tensor_tensor(span[:], extent_all[:, 0, :], extent_all[:, 1, :], ALU.add)\
                    .then_inc(s_chain_v, 1)
                nc.vector.tensor_scalar(base_f[:], extent_all[:, 0, :], -1.0, None, ALU.mult)\
                    .then_inc(s_chain_v, 1)
                chain[0] += 2
                dve.wait_ge(s_chain_v, chain[0])
                step(nc.vector.tensor_reduce(span_max[:], span[:, 0:GROUPS], AX, ALU.max))
                step(nc.vector.tensor_copy(span_i[:], span_max[:]))
                step(nc.vector.tensor_scalar(span_i[:], span_i[:], WINDOW.bit_length() - 1, None,
                                             ALU.logical_shift_right))
                step(nc.vector.tensor_scalar(choice_i[:, 0:1], span_i[:], 1.0, None, ALU.add))
                step(nc.vector.tensor_tensor(span[:], base_f[:], tile_due[:, 1:GROUPS + 2], ALU.subtract))
                step(nc.vector.tensor_reduce(slack[:], span[:, 0:GROUPS], AX, ALU.min))
                step(nc.vector.tensor_scalar(slack[:], slack[:], 0.0, None, ALU.is_ge))
                step(nc.vector.tensor_scalar(span_max[:], span_max[:], float(WINDOW), None, ALU.is_lt))
                step(nc.vector.tensor_tensor(choice_i[:, 1:2], slack[:], span_max[:], ALU.mult))

            @block.tensor
            def _(pe):
                pe.sem_inc(s_hot_used, GROUPS_PER_STEP)
                pe.wait_ge(s_const, 7)
                nc.tensor.matmul(bank[0][0:LO, 0:HI], zeros[:, 0:LO], zeros[:, 0:HI], start=True, stop=False)
                with pe.Fori(0, STEPS) as it:
                    for j in range(GROUPS_PER_STEP):
                        pe.wait_ge(s_hot, (it * GROUPS_PER_STEP + j) * 2 + 2)
                        for c in range(GROUP):
                            last = nc.tensor.matmul(bank[0][0:LO, 0:HI], onehot_lo[:, j, c], onehot_hi[:, j, c],
                                                    start=False, stop=False)
                        last.then_inc(s_hot_used, 1)
                nc.tensor.matmul(bank[0][0:LO, 0:HI], zeros[:, 0:LO], zeros[:, 0:HI], start=False, stop=True)\
                    .then_inc(s_deg, 1)
                pe.wait_ge(s_wt, 160)
                pe.sem_inc(s_xt, BATCH)
                pe.sem_inc(s_rows, 2)
                with pe.Fori(0, PASSES) as it:
                    for j in range(BATCH):
                        t = it * BATCH + j
                        pe.wait_ge(s_xn, t + 1)
                        for k in range(HALF):
                            last = nc.tensor.transpose(bank[1 + j % 2][:, k * P:(k + 1) * P],
                                                       buf_a[:, j, k * P:(k + 1) * P], ident[:])
                        last.then_inc(s_xn_t, 1)
                        pe.wait_ge(s_xt, t + 1 + BATCH)
                        pe.wait_ge(s_rows, t + (2 if j == 0 else 1))
                        for k in range(HALF):
                            last = nc.tensor.matmul(bank[3 + j % 2][:, 0:D], buf_b[:, j, k * P:(k + 1) * P],
                                                    w1_sb[:, k, :], start=(k == 0), stop=(k == HALF - 1))
                        last.then_inc(s_h, 1)

        setup_ctx.close()
        agg = sb("agg", [P, HALF, AGG])
        place = sb("place", [P, GROUPS_PER_STEP, GROUP, WINDOW])
        sum_rows = sb("sum_rows", [WINDOW, D])
        small = sb("small", [P, 66])
        top_u = sb("top_u", [P, 8], mybir.dt.uint32)
        comb_t = sb("comb_t", [EXPERTS, P])

        def write_first_table():
            s_g = sem("table_rows")
            s_gt = sem("table_rows_transposed")
            s_loops = sem("self_loops")
            s_store = [sem(f"table_store{j}") for j in range(BATCH)]
            s_stored = sem("table_stored")

            with nc.Block() as block:
                @block.sync
                def _(sp):
                    sp.sem_inc(s_stored, 1)
                    with sp.Fori(0, PASSES) as it:
                        for j in range(BATCH):
                            t = it * BATCH + j
                            sp.wait_ge(s_g, t + 1)
                            sp.dma_start(table_1[bass.ds(t * P, P), :], buf_a[:, j, :]).then_inc(s_store[j], 16)
                        for j in range(BATCH):
                            sp.wait_ge(s_store[j], it * 16 + 16)
                        sp.sem_inc(s_stored, 1)

                @block.scalar
                def _(act):
                    with act.Fori(0, PASSES) as it:
                        act.wait_ge(s_stored, it + 1)
                        act.wait_ge(s_gt, it * BATCH + 1)
                        for j in range(BATCH):
                            t = it * BATCH + j
                            nc.scalar.activation(buf_a[:, j, :], rows[:, bass.ds(t, 1), :]
                                                 .rearrange("p a b -> p (a b)"), ACT.Copy,
                                                 scale=dinv[:, bass.ds(t, 1)]).then_inc(s_g, 1)

                @block.vector
                def _(dve):
                    nc.vector.memset(agg[:, :, NODES:AGG], 0.0)
                    with dve.Fori(0, PASSES) as it:
                        for j in range(BATCH):
                            t = it * BATCH + j
                            dve.wait_ge(s_gt, t + 2)
                            nc.vector.tensor_copy(agg[:, :, bass.ds(t * P, P)],
                                                  bank[1 + j % 2][:, 0:D].rearrange("p (k n) -> p k n", k=HALF))\
                                .then_inc(s_loops, 1)

                @block.tensor
                def _(pe):
                    pe.sem_inc(s_gt, 1)
                    pe.sem_inc(s_loops, 2)
                    with pe.Fori(0, PASSES) as it:
                        for j in range(BATCH):
                            t = it * BATCH + j
                            pe.wait_ge(s_g, t + 1)
                            pe.wait_ge(s_loops, t + (2 if j == 0 else 1))
                            for k in range(HALF):
                                last = nc.tensor.transpose(bank[1 + j % 2][:, k * P:(k + 1) * P],
                                                           buf_a[:, j, k * P:(k + 1) * P], ident[:])
                            last.then_inc(s_gt, 1)

        def windows(tag):
            s_window = sem(f"windows_{tag}")

            def make(dve):
                nc.vector.tensor_copy(base_i[:], base_f[:]).then_inc(s_window, 1)
                nc.vector.tensor_tensor(dst_rel[:].rearrange("p (g c) -> p g c", c=GROUP),
                                        dst_f[:].rearrange("p (g c) -> p g c", c=GROUP),
                                        bc(base_f[:].unsqueeze(2), [P, GROUPS + 1, GROUP]),
                                        ALU.subtract).then_inc(s_window, 1)
                dve.wait_ge(s_window, 2)
            return make

        def edge_sums(tag, table):
            s_idx = [sem(f"indices_{tag}{j}") for j in range(GROUPS_PER_STEP)]
            s_row = [sem(f"rows_gathered_{tag}{j}") for j in range(GROUPS_PER_STEP)]
            s_eq = sem(f"edge_columns_{tag}")
            s_place = sem(f"placed_{tag}")
            s_sum = sem(f"group_summed_{tag}")
            s_copy = sem(f"sums_copied_{tag}")
            s_t = sem(f"sums_transposed_{tag}")
            s_add = sem(f"sums_added_{tag}")
            s_turn = sem(f"turn_{tag}")

            def sp_indices(sp, it, j, n):
                sp.wait_ge(s_sum, n + 1)
                sp.dma_start(idx[:, j, :], src[:, bass.ds(it * CHUNKS_PER_STEP + j * GROUP, GROUP)])\
                    .then_inc(s_idx[j], 16)

            def pool_gather(pool, j, step):
                pool.wait_ge(s_idx[j], step * 16 + 16)
                pool.sem_inc(s_turn, 1)
                for c in range(GROUP):
                    nc.gpsimd.indirect_dma_start(ring[:, j * GROUP + c, :], None, table,
                                                 bass.IndirectOffsetOnAxis(ap=idx[:, j, c:c + 1], axis=0))\
                        .then_inc(s_row[j], 16)

            def dve_place(dve, it, j, n):
                c = it * CHUNKS_PER_STEP + j * GROUP
                slot = place[:, j % GROUPS_PER_STEP]
                dve.wait_ge(s_sum, n + 1)
                nc.vector.tensor_tensor(slot, bc(iota[:, 0:WINDOW].unsqueeze(1), [P, GROUP, WINDOW]),
                                        bc(dst_rel[:, bass.ds(c, GROUP)].unsqueeze(2), [P, GROUP, WINDOW]),
                                        ALU.is_equal).then_inc(s_eq, 1)
                dve.wait_ge(s_eq, n + 1)
                nc.vector.tensor_tensor(slot, slot, bc(w_edge[:, bass.ds(c, GROUP)].unsqueeze(2),
                                                       [P, GROUP, WINDOW]), ALU.mult).then_inc(s_place, 1)

            def dve_add(dve, it, j, n):
                first = dve.value_load(base_i[0:1, bass.ds(it * GROUPS_PER_STEP + j, 1)], min_val=0, max_val=NODES)
                dve.wait_ge(s_t, n + 1)
                dve.wait_ge(s_add, n + 1)
                window = agg[:, :, bass.ds(first, WINDOW)]
                nc.vector.tensor_tensor(window, window, bank[1][:, 0:HALF * WINDOW]
                                        .rearrange("p (k n) -> p k n", k=HALF), ALU.add).then_inc(s_add, 1)

            def act_copy(act, n):
                act.wait_ge(s_sum, n + 1 + GROUPS_PER_STEP)
                nc.scalar.activation(sum_rows[:], bank[0][0:WINDOW, 0:D], ACT.Copy).then_inc(s_copy, 1)

            def pe_sum(pe, j, n, step):
                pe.wait_ge(s_place, n + 1)
                pe.wait_ge(s_row[j], step * (16 * GROUP) + 16 * GROUP)
                for c in range(GROUP):
                    last = nc.tensor.matmul(bank[0][0:WINDOW, 0:D], place[:, j, c], ring[:, j * GROUP + c, :],
                                            start=(c == 0), stop=(c == GROUP - 1))
                last.then_inc(s_sum, 1)

            def pe_transpose(pe, n):
                pe.wait_ge(s_copy, n + 1)
                pe.wait_ge(s_add, n + 1)
                pe.sem_inc(s_turn, 1)
                for k in range(HALF):
                    last = nc.tensor.transpose(bank[1][:, k * WINDOW:(k + 1) * WINDOW],
                                               sum_rows[:, k * P:(k + 1) * P], ident[0:WINDOW, 0:WINDOW])
                last.then_inc(s_t, 1)

            def act_wait_added(act, n):
                act.wait_ge(s_add, n + 2)

            parts = Parts()
            parts.sp_indices = sp_indices
            parts.pool_gather = pool_gather
            parts.dve_place = dve_place
            parts.dve_add = dve_add
            parts.act_copy = act_copy
            parts.pe_sum = pe_sum
            parts.pe_transpose = pe_transpose
            parts.act_wait_added = act_wait_added
            parts.s_add = s_add
            parts.s_sum = s_sum
            parts.s_turn = s_turn
            return parts

        def sum_edges_in_rounds(tag, table, rounds):
            make_windows = windows(tag)
            e = edge_sums(tag, table)
            s_next = sem(f"next_round_{tag}")
            with nc.Block() as block:
                @block.vector
                def _(dve):
                    make_windows(dve)
                    dve.sem_inc(e.s_add, 1)

                @block.tensor
                def _(pe):
                    pe.sem_inc(e.s_sum, GROUPS_PER_STEP)

            with nc.Fori(0, rounds) as rnd:
                with nc.Block() as block:
                    def steps(eng):
                        with eng.Fori(0, STEPS) as it:
                            for j in range(GROUPS_PER_STEP):
                                step = rnd * STEPS + it
                                yield it, j, step, step * GROUPS_PER_STEP + j

                    @block.sync
                    def _(sp):
                        for it, j, step, n in steps(sp):
                            e.sp_indices(sp, it, j, n)

                    @block.gpsimd
                    def _(pool):
                        for it, j, step, n in steps(pool):
                            e.pool_gather(pool, j, step)

                    @block.vector
                    def _(dve):
                        for it, j, step, n in steps(dve):
                            e.dve_place(dve, it, j, n)
                            e.dve_add(dve, it, j, n)
                        nc.vector.tensor_scalar(base_i[:], base_i[:], float(WINDOW), float(NODES), ALU.add,
                                                ALU.min).then_inc(s_next, 1)
                        nc.vector.tensor_scalar(dst_rel[:], dst_rel[:], -float(WINDOW), None, ALU.add)\
                            .then_inc(s_next, 1)
                        dve.wait_ge(s_next, rnd * 2 + 2)
                        dve.sem_inc(e.s_turn, 1)

                    @block.scalar
                    def _(act):
                        for it, j, step, n in steps(act):
                            e.act_copy(act, n)

                    @block.tensor
                    def _(pe):
                        for it, j, step, n in steps(pe):
                            e.pe_sum(pe, j, n, step)
                            e.pe_transpose(pe, n)

        def second_table(tag):
            relu_t, biased, table_row = buf_a[:, 0, :], buf_a[:, 1, :], buf_a[:, 2, :]
            s_relu = sem(f"mid_relu_{tag}")
            s_u = sem(f"mid_product_{tag}")
            s_v = sem(f"mid_biased_{tag}")
            s_g = sem(f"mid_rows_{tag}")
            s_gt = sem(f"mid_transposed_{tag}")
            s_loop = sem(f"mid_self_loops_{tag}")
            s_store = sem(f"mid_store_{tag}")

            def act_relu(act, m):
                nc.scalar.activation(relu_t.rearrange("p (k n) -> p k n", k=HALF), agg[:, :, bass.ds(m * P, P)],
                                     ACT.Relu).then_inc(s_relu, 1)

            def pe_product(pe, m):
                pe.wait_ge(s_relu, m + 1)
                for k in range(HALF):
                    last = nc.tensor.matmul(bank[2][:, 0:D], relu_t[:, k * P:(k + 1) * P], w2_sb[:, k, :],
                                            start=(k == 0), stop=(k == HALF - 1))
                last.then_inc(s_u, 1)

            def dve_bias(dve, m):
                dve.wait_ge(s_u, m + 1)
                nc.vector.scalar_tensor_tensor(biased, bank[2][:, 0:D], dinv[:, bass.ds(m, 1)], b2_sb[:],
                                               ALU.mult, ALU.add).then_inc(s_v, 1)

            def act_row(act, m):
                act.wait_ge(s_v, m + 1)
                nc.scalar.activation(table_row, biased, ACT.Copy, scale=dinv[:, bass.ds(m, 1)]).then_inc(s_g, 1)
                act.wait_ge(s_g, m + 1)
                act.dma_start(table_2[bass.ds(m * P, P), :], table_row).then_inc(s_store, 16)

            def act_stored(act, m):
                act.wait_ge(s_store, m * 16 + 16)
                act.wait_ge(s_gt, m + 1)

            def pe_transpose(pe, m):
                pe.wait_ge(s_g, m + 1)
                for k in range(HALF):
                    last = nc.tensor.transpose(bank[3][:, k * P:(k + 1) * P], table_row[:, k * P:(k + 1) * P],
                                               ident[:])
                last.then_inc(s_gt, 1)

            def dve_self_loops(dve, m):
                dve.wait_ge(s_gt, m + 1)
                nc.vector.tensor_copy(agg[:, :, bass.ds(m * P, P)],
                                      bank[3][:, 0:D].rearrange("p (k n) -> p k n", k=HALF)).then_inc(s_loop, 1)

            def pe_self_loops_done(pe, m):
                pe.wait_ge(s_loop, m + 1)

            parts = Parts()
            parts.act_relu = act_relu
            parts.pe_product = pe_product
            parts.dve_bias = dve_bias
            parts.act_row = act_row
            parts.act_stored = act_stored
            parts.pe_transpose = pe_transpose
            parts.dve_self_loops = dve_self_loops
            parts.pe_self_loops_done = pe_self_loops_done
            return parts

        def expert_tiles(tag):
            x_in, x1, y, x1_y, y_t, total, relu_t = [buf_a[:, i, :] for i in range(7)]
            hidden = [buf_b[:, i, :] for i in range(2)]
            rows_p, y_t_p = bank[2][:, 0:D], bank[2][:, D:2 * D]
            logits_p, comb_t_p, bias_p = bank[3][:, 0:EXPERTS], bank[3][0:EXPERTS, P:2 * P], bank[3][:, D:2 * D]
            hidden_p = [bank[4][:, 0:D], bank[5][:, 0:D]]
            expert_p = [bank[6][:, 0:D], bank[7][:, 0:D]]
            mstat, mv = small[:, 0:6], small[:, 6:8]
            inv_std, neg_mean = small[:, 8:9], small[:, 9:10]
            neg_max, exp_sum, exp_inv = small[:, 10:11], small[:, 11:12], small[:, 12:13]
            pair_sum, pair_inv, top_w = small[:, 13:14], small[:, 14:15], small[:, 16:18]
            top_i, prob, top_p = small[:, 18:26], small[:, 26:34], small[:, 34:42]
            comb_0, comb_1, comb = small[:, 42:50], small[:, 50:58], small[:, 58:66]

            s_x = sem(f"tile_loaded_{tag}")
            s_relu = sem(f"tile_relu_{tag}")
            s_rows = sem(f"tile_rows_{tag}")
            s_x1 = sem(f"tile_residual_{tag}")
            s_var = sem(f"tile_variance_{tag}")
            s_std = sem(f"tile_deviation_{tag}")
            s_y = sem(f"tile_normalised_{tag}")
            s_yt = sem(f"tile_transposed_{tag}")
            s_yt_sb = sem(f"tile_transposed_copied_{tag}")
            s_logit = sem(f"logits_{tag}")
            s_nmax = sem(f"logit_max_{tag}")
            s_exp = sem(f"logit_exp_{tag}")
            s_comb = sem(f"combine_ready_{tag}")
            s_comb_t = sem(f"combine_transposed_{tag}")
            s_comb_sb = sem(f"combine_copied_{tag}")
            s_bias = sem(f"combined_bias_{tag}")
            s_hid = sem(f"hidden_product_{tag}")
            s_gelu = sem(f"hidden_ready_{tag}")
            s_exp_y = sem(f"expert_product_{tag}")
            s_acc = sem(f"expert_added_{tag}")
            s_store = sem(f"tile_store_{tag}")
            s_chain = sem(f"expert_vector_step_{tag}")
            chain = [0]

            def chain_restart(dve):
                dve.sem_clear(s_chain)
                chain[0] = 0

            def step(dve, ins):
                chain[0] += 1
                ins.then_inc(s_chain, 1)
                dve.wait_ge(s_chain, chain[0])

            def credits(pe):
                pe.sem_inc(s_hid, 1)
                pe.sem_inc(s_exp_y, 2)
                pe.sem_inc(s_acc, 2)

            def sp_load(sp, m, first=False):
                if not first:
                    sp.wait_ge(s_x1, m)
                sp.dma_start(x_in, x[bass.ds(m * P, P), :]).then_inc(s_x, 16)

            def act_relu(act, m, first=False):
                if not first:
                    act.wait_ge(s_rows, m)
                nc.scalar.activation(relu_t.rearrange("p (k n) -> p k n", k=HALF),
                                     agg[:, :, bass.ds(m * P, P)], ACT.Relu).then_inc(s_relu, 1)

            def pe_rows(pe, m):
                pe.wait_ge(s_relu, m + 1)
                for k in range(HALF):
                    last = nc.tensor.transpose(rows_p[:, k * P:(k + 1) * P], relu_t[:, k * P:(k + 1) * P], ident[:])
                last.then_inc(s_rows, 1)

            def dve_residual(dve, m):
                dve.wait_ge(s_rows, m + 1)
                dve.wait_ge(s_x, m * 16 + 16)
                nc.vector.scalar_tensor_tensor(x1, rows_p, dinv[:, bass.ds(m, 1)], x_in, ALU.mult,
                                               ALU.add).then_inc(s_x1, 1)
                dve.wait_ge(s_x1, m + 1)
                step(dve, nc.vector.bn_stats(mstat, x1))
                nc.vector.bn_aggr(mv, mstat).then_inc(s_var, 1)

            def act_std(act, m):
                act.wait_ge(s_var, m + 1)
                nc.scalar.activation(inv_std, mv[:, 1:2], ACT.Sqrt, bias=eps[:, 0:1]).then_inc(s_std, 1)

            def dve_normalise(dve, m, first=False):
                dve.wait_ge(s_std, m + 1)
                step(dve, nc.vector.reciprocal(inv_std, inv_std))
                step(dve, nc.vector.scalar_tensor_tensor(neg_mean, mv[:, 0:1], -1.0, inv_std, ALU.mult, ALU.mult))
                if not first:
                    dve.wait_ge(s_yt, m)
                nc.vector.tensor_scalar(y, x1, inv_std, neg_mean, ALU.mult, ALU.add).then_inc(s_y, 1)
                dve.wait_ge(s_y, m + 1)
                step(dve, nc.vector.tensor_tensor(x1_y, x1, y, ALU.add))

            def pe_y(pe, m, first=False):
                pe.wait_ge(s_y, m + 1)
                if not first:
                    pe.wait_ge(s_yt_sb, m)
                for k in range(HALF):
                    last = nc.tensor.transpose(y_t_p[:, k * P:(k + 1) * P], y[:, k * P:(k + 1) * P], ident[:])
                last.then_inc(s_yt, 1)

            def act_y_t(act, t):
                act.wait_ge(s_yt, t + 1)
                act.wait_ge(s_hid, t * EXPERTS + 1)
                nc.scalar.activation(y_t, y_t_p, ACT.Copy).then_inc(s_yt_sb, 1)

            def pe_logits(pe, t):
                pe.wait_ge(s_yt_sb, t + 1)
                for k in range(HALF):
                    last = nc.tensor.matmul(logits_p, y_t[:, k * P:(k + 1) * P], router_sb[:, k, :],
                                            start=(k == 0), stop=(k == 1))
                last.then_inc(s_logit, 1)

            def dve_logit_max(dve, t):
                dve.wait_ge(s_logit, t + 1)
                nc.vector.tensor_reduce(neg_max, logits_p, AX, ALU.max, negate=True).then_inc(s_nmax, 1)

            def act_exp(act, t):
                act.wait_ge(s_nmax, t + 1)
                nc.scalar.activation(prob, logits_p, ACT.Exp, bias=neg_max, accum_out=exp_sum).then_inc(s_exp, 1)

            def dve_combine(dve, t):
                dve.wait_ge(s_exp, t + 1)
                step(dve, nc.vector.reciprocal(exp_inv, exp_sum))
                step(dve, nc.vector.tensor_scalar(prob, prob, exp_inv, None, ALU.mult))
                step(dve, nc.vector.max(top_p, prob))
                step(dve, nc.vector.max_index(top_u[:], top_p, prob))
                step(dve, nc.vector.tensor_copy(top_i, top_u[:]))
                step(dve, nc.vector.tensor_tensor(pair_sum, top_p[:, 0:1], top_p[:, 1:2], ALU.add))
                step(dve, nc.vector.tensor_scalar(pair_sum, pair_sum, 1e-12, None, ALU.max))
                step(dve, nc.vector.reciprocal(pair_inv, pair_sum))
                step(dve, nc.vector.tensor_scalar(top_w, top_p[:, 0:2], pair_inv, None, ALU.mult))
                step(dve, nc.vector.tensor_scalar(comb_0, iota[:, 0:EXPERTS], top_i[:, 0:1], top_w[:, 0:1],
                                                  ALU.is_equal, ALU.mult))
                step(dve, nc.vector.tensor_scalar(comb_1, iota[:, 0:EXPERTS], top_i[:, 1:2], top_w[:, 1:2],
                                                  ALU.is_equal, ALU.mult))
                nc.vector.tensor_tensor(comb, comb_0, comb_1, ALU.add).then_inc(s_comb, 1)

            def pe_combine_t(pe, t):
                pe.wait_ge(s_comb, t + 1)
                nc.tensor.transpose(comb_t_p, comb, ident[:]).then_inc(s_comb_t, 1)

            def act_combine_t(act, t):
                act.wait_ge(s_comb_t, t + 1)
                nc.scalar.activation(comb_t[:], comb_t_p, ACT.Copy).then_inc(s_comb_sb, 1)

            def pe_bias(pe, t):
                pe.wait_ge(s_comb_sb, t + 1)
                nc.tensor.matmul(bias_p, comb_t[:], moe_b2_sb[:], start=True, stop=True).then_inc(s_bias, 1)

            def dve_total(dve, t):
                dve.wait_ge(s_bias, t + 1)
                step(dve, nc.vector.tensor_tensor(total, bias_p, x1_y, ALU.add))

            def pe_hidden(pe, t, e):
                for f in range(HALF):
                    for k in range(HALF):
                        last = nc.tensor.matmul(hidden_p[e % 2][:, f * P:(f + 1) * P],
                                                moe_w1_sb[:, e, k, f * P:(f + 1) * P],
                                                y_t[:, k * P:(k + 1) * P], start=(k == 0), stop=(k == 1))
                last.then_inc(s_hid, 1)

            def act_gelu(act, t, e):
                act.wait_ge(s_hid, t * EXPERTS + e + 2)
                act.wait_ge(s_exp_y, t * EXPERTS + e + 1)
                for k in range(HALF):
                    nc.scalar.activation(hidden[e % 2][:, k * P:(k + 1) * P],
                                         hidden_p[e % 2][:, k * P:(k + 1) * P], ACT.Gelu,
                                         bias=moe_b1_sb[:, e * HALF + k:e * HALF + k + 1]).then_inc(s_gelu, 1)

            def pe_expert(pe, t, e):
                pe.wait_ge(s_gelu, (t * EXPERTS + e) * HALF + HALF)
                pe.wait_ge(s_acc, t * EXPERTS + e + 1)
                for f in range(HALF):
                    last = nc.tensor.matmul(expert_p[e % 2], hidden[e % 2][:, f * P:(f + 1) * P],
                                            moe_w2_sb[:, e, f, :], start=(f == 0), stop=(f == 1))
                last.then_inc(s_exp_y, 1)

            def dve_expert(dve, t, e):
                dve.wait_ge(s_exp_y, t * EXPERTS + e + 3)
                dve.wait_ge(s_acc, t * EXPERTS + e + 2)
                nc.vector.scalar_tensor_tensor(total, expert_p[e % 2], comb[:, e:e + 1], total,
                                               ALU.mult, ALU.add).then_inc(s_acc, 1)

            def act_store(act, t):
                act.wait_ge(s_acc, (t + 1) * EXPERTS + 2)
                act.dma_start(out[bass.ds(t * P, P), :], total).then_inc(s_store, 16)

            def dve_stored(dve, t):
                dve.wait_ge(s_store, t * 16 + 16)

            parts = Parts()
            parts.chain_restart = chain_restart
            parts.credits = credits
            parts.sp_load = sp_load
            parts.act_relu = act_relu
            parts.pe_rows = pe_rows
            parts.dve_residual = dve_residual
            parts.act_std = act_std
            parts.dve_normalise = dve_normalise
            parts.pe_y = pe_y
            parts.act_y_t = act_y_t
            parts.pe_logits = pe_logits
            parts.dve_logit_max = dve_logit_max
            parts.act_exp = act_exp
            parts.dve_combine = dve_combine
            parts.pe_combine_t = pe_combine_t
            parts.act_combine_t = act_combine_t
            parts.pe_bias = pe_bias
            parts.dve_total = dve_total
            parts.pe_hidden = pe_hidden
            parts.act_gelu = act_gelu
            parts.pe_expert = pe_expert
            parts.dve_expert = dve_expert
            parts.act_store = act_store
            parts.dve_stored = dve_stored
            return parts

        def second_table_alone():
            m_ = second_table("alone")
            with nc.Block() as block:
                @block.scalar
                def _(act):
                    with act.Fori(0, TILES) as m:
                        m_.act_relu(act, m)
                        m_.act_row(act, m)
                        m_.act_stored(act, m)

                @block.vector
                def _(dve):
                    with dve.Fori(0, TILES) as m:
                        m_.dve_bias(dve, m)
                        m_.dve_self_loops(dve, m)

                @block.tensor
                def _(pe):
                    with pe.Fori(0, TILES) as m:
                        m_.pe_product(pe, m)
                        m_.pe_transpose(pe, m)
                        m_.pe_self_loops_done(pe, m)

        def act_tile(act, x_, t):
            x_.act_y_t(act, t)
            x_.act_exp(act, t)
            x_.act_relu(act, t + 1)
            x_.act_gelu(act, t, 0)
            x_.act_gelu(act, t, 1)
            x_.act_combine_t(act, t)
            x_.act_gelu(act, t, 2)
            x_.act_gelu(act, t, 3)
            x_.act_gelu(act, t, 4)
            x_.act_std(act, t + 1)
            x_.act_gelu(act, t, 5)
            x_.act_gelu(act, t, 6)
            x_.act_gelu(act, t, 7)
            x_.act_store(act, t)

        def dve_tile(dve, x_, t):
            x_.chain_restart(dve)
            x_.dve_logit_max(dve, t)
            x_.dve_combine(dve, t)
            x_.dve_total(dve, t)
            x_.dve_expert(dve, t, 0)
            x_.dve_expert(dve, t, 1)
            x_.dve_residual(dve, t + 1)
            x_.dve_expert(dve, t, 2)
            x_.dve_expert(dve, t, 3)
            x_.dve_normalise(dve, t + 1)
            for e in range(4, EXPERTS):
                x_.dve_expert(dve, t, e)
            x_.dve_stored(dve, t)

        def pe_tile(pe, x_, t):
            x_.pe_logits(pe, t)
            x_.pe_hidden(pe, t, 0)
            x_.pe_hidden(pe, t, 1)
            x_.pe_rows(pe, t + 1)
            x_.pe_combine_t(pe, t)
            x_.pe_expert(pe, t, 0)
            x_.pe_bias(pe, t)
            for e in range(2, EXPERTS):
                x_.pe_hidden(pe, t, e)
                x_.pe_expert(pe, t, e - 1)
                if e == 6:
                    x_.pe_y(pe, t + 1)
            x_.pe_expert(pe, t, EXPERTS - 1)

        def experts_alone():
            x_ = expert_tiles("alone")
            with nc.Block() as block:
                @block.sync
                def _(sp):
                    x_.sp_load(sp, 0, first=True)
                    with sp.Fori(0, TILES) as t:
                        x_.sp_load(sp, t + 1)

                @block.scalar
                def _(act):
                    x_.act_relu(act, 0, first=True)
                    x_.act_std(act, 0)
                    with act.Fori(0, TILES) as t:
                        act_tile(act, x_, t)

                @block.vector
                def _(dve):
                    x_.dve_residual(dve, 0)
                    x_.dve_normalise(dve, 0, first=True)
                    with dve.Fori(0, TILES) as t:
                        dve_tile(dve, x_, t)

                @block.tensor
                def _(pe):
                    x_.credits(pe)
                    x_.pe_rows(pe, 0)
                    x_.pe_y(pe, 0, first=True)
                    with pe.Fori(0, TILES) as t:
                        pe_tile(pe, x_, t)

        def group_number(it, j):
            return it * GROUPS_PER_STEP + j

        def first_layer_beside_table():
            make_windows = windows("fast1")
            e = edge_sums("fast1", table_1)
            m_ = second_table("fast1")
            with nc.Block() as block:
                @block.sync
                def _(sp):
                    with sp.Fori(0, STEPS) as it:
                        for j in range(GROUPS_PER_STEP):
                            e.sp_indices(sp, it, j, group_number(it, j))

                @block.gpsimd
                def _(pool):
                    with pool.Fori(0, STEPS) as it:
                        for j in range(GROUPS_PER_STEP):
                            e.pool_gather(pool, j, it)

                @block.vector
                def _(dve):
                    def groups(it, m):
                        for j in range(GROUPS_PER_STEP):
                            e.dve_place(dve, it, j + 1, group_number(it, j + 1))
                            e.dve_add(dve, it, j, group_number(it, j))
                        if m is not None:
                            m_.dve_bias(dve, m)
                            m_.dve_self_loops(dve, m)

                    make_windows(dve)
                    dve.sem_inc(e.s_add, 1)
                    e.dve_place(dve, 0, 0, 0)
                    groups(0, None)
                    with dve.Fori(1, STEPS) as it:
                        groups(it, it - 1)
                    m_.dve_bias(dve, TILES - 1)
                    m_.dve_self_loops(dve, TILES - 1)

                @block.scalar
                def _(act):
                    def tile(m):
                        m_.act_relu(act, m)
                        m_.act_row(act, m)
                        m_.act_stored(act, m)

                    for j in range(GROUPS_PER_STEP):
                        e.act_copy(act, j)
                    with act.Fori(1, STEPS) as it:
                        for j in range(GROUPS_PER_STEP):
                            e.act_copy(act, group_number(it, j))
                        e.act_wait_added(act, group_number(it, 1))
                        tile(it - 1)
                    e.act_wait_added(act, GROUPS - 1)
                    tile(TILES - 1)

                @block.tensor
                def _(pe):
                    def groups(it):
                        for j in range(GROUPS_PER_STEP):
                            e.pe_sum(pe, j, group_number(it, j), it)
                            e.pe_transpose(pe, group_number(it, j))

                    def tile(m):
                        m_.pe_product(pe, m)
                        m_.pe_transpose(pe, m)
                        m_.pe_self_loops_done(pe, m)

                    pe.sem_inc(e.s_sum, GROUPS_PER_STEP)
                    groups(0)
                    with pe.Fori(1, STEPS) as it:
                        groups(it)
                        tile(it - 1)
                    tile(TILES - 1)

        def second_layer_beside_experts():
            make_windows = windows("fast2")
            e = edge_sums("fast2", table_2)
            x_ = expert_tiles("fast2")
            LEAD = 2
            with nc.Block() as block:
                @block.sync
                def _(sp):
                    with sp.Fori(0, LEAD) as it:
                        for j in range(GROUPS_PER_STEP):
                            e.sp_indices(sp, it, j, group_number(it, j))
                    x_.sp_load(sp, 0, first=True)
                    with sp.Fori(LEAD, STEPS) as it:
                        e.sp_indices(sp, it, 0, group_number(it, 0))
                        e.sp_indices(sp, it, 1, group_number(it, 1))
                        x_.sp_load(sp, it - 1)
                        e.sp_indices(sp, it, 2, group_number(it, 2))
                    with sp.Fori(TILES - LEAD, TILES) as t:
                        x_.sp_load(sp, t + 1)

                @block.gpsimd
                def _(pool):
                    with pool.Fori(0, STEPS) as it:
                        for j in range(GROUPS_PER_STEP):
                            e.pool_gather(pool, j, it)

                @block.scalar
                def _(act):
                    for n in range(LEAD * GROUPS_PER_STEP):
                        e.act_copy(act, n)
                    e.act_wait_added(act, LEAD * GROUPS_PER_STEP - 1)
                    x_.act_relu(act, 0, first=True)
                    x_.act_std(act, 0)
                    with act.Fori(LEAD, STEPS) as it:
                        t = it - LEAD
                        x_.act_y_t(act, t)
                        e.act_copy(act, group_number(it, 0))
                        x_.act_exp(act, t)
                        x_.act_gelu(act, t, 0)
                        x_.act_gelu(act, t, 1)
                        x_.act_gelu(act, t, 2)
                        x_.act_combine_t(act, t)
                        e.act_copy(act, group_number(it, 1))
                        x_.act_gelu(act, t, 3)
                        x_.act_gelu(act, t, 4)
                        e.act_wait_added(act, group_number(it, 1))
                        x_.act_relu(act, it - 1)
                        x_.act_gelu(act, t, 5)
                        x_.act_std(act, it - 1)
                        e.act_copy(act, group_number(it, 2))
                        x_.act_gelu(act, t, 6)
                        x_.act_gelu(act, t, 7)
                        x_.act_store(act, t)
                    e.act_wait_added(act, GROUPS - 1)
                    with act.Fori(TILES - LEAD, TILES) as t:
                        act_tile(act, x_, t)

                @block.vector
                def _(dve):
                    def place_next(it, j):
                        e.dve_place(dve, it, j + 1, group_number(it, j + 1))

                    def add(it, j):
                        e.dve_add(dve, it, j, group_number(it, j))

                    make_windows(dve)
                    dve.sem_inc(e.s_add, 1)
                    e.dve_place(dve, 0, 0, 0)
                    with dve.Fori(0, LEAD) as it:
                        for j in range(GROUPS_PER_STEP):
                            place_next(it, j)
                            add(it, j)
                    x_.dve_residual(dve, 0)
                    x_.dve_normalise(dve, 0, first=True)
                    with dve.Fori(LEAD, STEPS) as it:
                        t = it - LEAD
                        x_.chain_restart(dve)
                        place_next(it, 0)
                        x_.dve_logit_max(dve, t)
                        add(it, 0)
                        x_.dve_combine(dve, t)
                        x_.dve_total(dve, t)
                        x_.dve_expert(dve, t, 0)
                        x_.dve_expert(dve, t, 1)
                        place_next(it, 1)
                        x_.dve_expert(dve, t, 2)
                        add(it, 1)
                        x_.dve_expert(dve, t, 3)
                        x_.dve_expert(dve, t, 4)
                        x_.dve_residual(dve, it - 1)
                        place_next(it, 2)
                        x_.dve_normalise(dve, it - 1)
                        x_.dve_expert(dve, t, 5)
                        add(it, 2)
                        x_.dve_expert(dve, t, 6)
                        x_.dve_expert(dve, t, 7)
                        x_.dve_stored(dve, t)
                    with dve.Fori(TILES - LEAD, TILES) as t:
                        dve_tile(dve, x_, t)

                @block.tensor
                def _(pe):
                    def summed(it, j):
                        e.pe_sum(pe, j, group_number(it, j), it)

                    def transposed(it, j):
                        e.pe_transpose(pe, group_number(it, j))

                    pe.sem_inc(e.s_sum, GROUPS_PER_STEP)
                    x_.credits(pe)
                    with pe.Fori(0, LEAD) as it:
                        for j in range(GROUPS_PER_STEP):
                            summed(it, j)
                            transposed(it, j)
                    x_.pe_rows(pe, 0)
                    x_.pe_y(pe, 0, first=True)
                    with pe.Fori(LEAD, STEPS) as it:
                        t = it - LEAD
                        summed(it, 0)
                        x_.pe_logits(pe, t)
                        x_.pe_hidden(pe, t, 0)
                        x_.pe_hidden(pe, t, 1)
                        transposed(it, 0)
                        x_.pe_expert(pe, t, 0)
                        x_.pe_hidden(pe, t, 2)
                        x_.pe_expert(pe, t, 1)
                        x_.pe_combine_t(pe, t)
                        x_.pe_bias(pe, t)
                        summed(it, 1)
                        x_.pe_hidden(pe, t, 3)
                        x_.pe_expert(pe, t, 2)
                        transposed(it, 1)
                        x_.pe_hidden(pe, t, 4)
                        x_.pe_expert(pe, t, 3)
                        x_.pe_hidden(pe, t, 5)
                        x_.pe_expert(pe, t, 4)
                        x_.pe_rows(pe, it - 1)
                        summed(it, 2)
                        x_.pe_hidden(pe, t, 6)
                        x_.pe_expert(pe, t, 5)
                        transposed(it, 2)
                        x_.pe_hidden(pe, t, 7)
                        x_.pe_expert(pe, t, 6)
                        x_.pe_y(pe, it - 1)
                        x_.pe_expert(pe, t, 7)
                    with pe.Fori(TILES - LEAD, TILES) as t:
                        pe_tile(pe, x_, t)

        write_first_table()
        rounds = nc.values_load(choice_i[0:1, 0:1], min_val=1, max_val=NODES // WINDOW + 1)
        spread = nc.values_load(choice_i[0:1, 1:2], min_val=0, max_val=1)
        with nc.If(spread == 1):
            first_layer_beside_table()
            second_layer_beside_experts()
        with nc.Else():
            sum_edges_in_rounds("r1", table_1, rounds)
            second_table_alone()
            sum_edges_in_rounds("r2", table_2, rounds)
            experts_alone()


def lay_out(x, src, dst, edge_weight1, L0_gnn_W1, L0_gnn_b1, L0_gnn_W2, L0_gnn_b2,
           L0_ffn_router_w, L0_ffn_w1, L0_ffn_b1, L0_ffn_w2, L0_ffn_b2):
    import numpy as np

    def by_partition(edges, fill):
        flat = np.full(CHUNKS_PAD * P, fill, edges.dtype)
        flat[:N_EDGES] = edges
        return flat.reshape(CHUNKS_PAD, P).T

    x = np.asarray(x)
    x_pad = np.zeros((TILES_PAD * P, D), x.dtype)
    x_pad[:N_NODES] = x
    b1 = np.asarray(L0_ffn_b1).reshape(EXPERTS * HALF, P).T
    ins = {
        "x": x_pad,
        "src": by_partition(np.asarray(src), 0),
        "dst": by_partition(np.asarray(dst), N_NODES),
        "weight": by_partition(np.asarray(edge_weight1)[:, 0], 0),
        "gnn_w1": np.asarray(L0_gnn_W1).T, "gnn_b1": np.asarray(L0_gnn_b1),
        "gnn_w2": np.asarray(L0_gnn_W2).T, "gnn_b2": np.asarray(L0_gnn_b2),
        "router": np.asarray(L0_ffn_router_w).T,
        "moe_w1": np.asarray(L0_ffn_w1), "moe_b1": b1,
        "moe_w2": np.asarray(L0_ffn_w2), "moe_b2": np.asarray(L0_ffn_b2),
    }
    return {f"in_{n}": np.ascontiguousarray(a) for n, a in ins.items()}


def kernel(**inputs):
    import concourse.bacc as bacc
    from concourse.bass_utils import run_bass_kernel_spmd

    ins = lay_out(**inputs)
    nc = bacc.Bacc("TRN2", target_bir_lowering=False, num_devices=1)
    args = [nc.dram_tensor(n, a.shape, mybir.dt.from_np(a.dtype), kind="ExternalInput").ap() for n, a in ins.items()]
    out = nc.dram_tensor("out_rows", (NODES, D), F32, kind="ExternalOutput").ap()
    gnn_ffn_kernel(nc, *args, out)
    r = run_bass_kernel_spmd(nc, [ins], core_ids=[0])
    return r.results[0]["out_rows"][:N_NODES]
```

```python
import concourse.bass as bass
from concourse import mybir
from contextlib import ExitStack

F32 = mybir.dt.float32
F16 = mybir.dt.float16
I32 = mybir.dt.int32
ALU = mybir.AluOpType
ACT = mybir.ActivationFunctionType
AX = mybir.AxisListType.X

P = 128
D = 256
HALF = D // P
N_NODES = 6250
N_EDGES = 206250
EXPERTS = 8
TILES = -(-N_NODES // P)
NODES = TILES * P
TILES_PAD = TILES + 1
GROUP = 11
EARLY = 8
GROUPS_PER_STEP = 3
STEPS = TILES
CHUNKS_PER_STEP = GROUP * GROUPS_PER_STEP
CHUNKS = STEPS * CHUNKS_PER_STEP
GROUPS = STEPS * GROUPS_PER_STEP
CHUNKS_PAD = CHUNKS + GROUP
assert CHUNKS * P >= N_EDGES
WINDOW = 64
AGG = TILES_PAD * P
COUNTED_TOGETHER = 4
LO = 64
HI = NODES // LO
BATCH = 7
PASSES = TILES // BATCH
LOW = 8
HIGHS = WINDOW // LOW + 1
HIGHS_OF_TILE = P // LOW
PART = BATCH
PARTS = GROUPS // PART
PARTS_PER_ROUND = 3
BLOCK = HIGHS * GROUP
PAD = P - LOW
assert P % LOW == 0 and PARTS % PARTS_PER_ROUND == 0 and GROUP * P <= 2048 and \
    COUNTED_TOGETHER * BLOCK <= 512
assert BATCH * PASSES == TILES and HI * LO == NODES and HI == 2 * TILES
EPS = 1e-5
RMAX = bass.bass_isa.ReduceOp.max


class Parts:
    pass


def gnn_ffn_kernel(nc, x, src, dst, weight, gnn_w1, gnn_b1, gnn_w2, gnn_b2,
                   router, moe_w1, moe_b1, moe_w2, moe_b2, out):
    ctx = ExitStack()
    with ctx:
        def sb(name, shape, dt=F32):
            return ctx.enter_context(nc.sbuf_tensor(name, shape, dt))

        semaphores = {}

        def sem(name):
            if name not in semaphores:
                semaphores[name] = ctx.enter_context(nc.semaphore(name))
            return semaphores[name]

        table_1 = nc.dram_tensor("table_1", [NODES, D], F32, kind="Internal").ap()
        table_2 = nc.dram_tensor("table_2", [NODES, D], F32, kind="Internal").ap()
        table_1_tiles = table_1.rearrange("(t p) d -> p t d", p=P)
        x_tiles = x.rearrange("(t p) d -> p t d", p=P)

        rows = sb("rows", [P, TILES, D])
        ring = rows[:, 0:CHUNKS_PER_STEP, :]
        dst_f = sb("dst_f", [P, CHUNKS_PAD])
        dst_rel = sb("dst_rel", [P, CHUNKS_PAD])
        w_edge = sb("w_edge", [P, CHUNKS_PAD])
        idx = sb("idx", [P, 2, GROUPS_PER_STEP, GROUP], I32)
        base_f = sb("base_f", [P, GROUPS + 1])
        base_i = sb("base_i", [P, GROUPS + 1], I32)
        choice_i = sb("choice_i", [P, 2], I32)
        iota = sb("iota", [P, P])
        ident = sb("ident", [P, P])
        w1_sb = sb("w1_sb", [P, HALF, D])
        w2_sb = sb("w2_sb", [P, HALF, D])
        b1_sb = sb("b1_sb", [P, D])
        b2_sb = sb("b2_sb", [P, D])
        router_sb = sb("router_sb", [P, HALF, EXPERTS])
        moe_w1_sb = sb("moe_w1_sb", [P, EXPERTS, HALF, D])
        moe_w2_sb = sb("moe_w2_sb", [P, EXPERTS, HALF, D])
        moe_b1_sb = sb("moe_b1_sb", [P, EXPERTS * HALF])
        moe_b2_sb = sb("moe_b2_sb", [EXPERTS, D])
        eps = sb("eps", [P, 1])
        dinv = sb("dinv", [P, TILES_PAD])
        rstd = sb("rstd", [P, TILES])
        shift = sb("shift", [P, TILES])
        buf_a = sb("buf_a", [P, BATCH, D])
        buf_b = sb("buf_b", [P, BATCH, D])

        bank = [ctx.enter_context(nc.psum_tensor(f"bank{i}", [P, 512], F32)) for i in range(8)]

        bc = lambda ap, shape: ap.to_broadcast(shape)

        setup_ctx = ExitStack()

        def tmp(name, shape, dt=F32, within=setup_ctx):
            return within.enter_context(nc.sbuf_tensor(name, shape, dt))

        dst_i = tmp("dst_i", [P, CHUNKS_PAD], I32)
        extent = tmp("extent", [P, 2, GROUPS + 1])
        extent_all = tmp("extent_all", [P, 2, GROUPS + 1])
        span = tmp("span", [P, GROUPS + 1])
        span_max = tmp("span_max", [P, 1])
        span_i = tmp("span_i", [P, 1], I32)
        slack = tmp("slack", [P, GROUPS + 1])
        slack_min = tmp("slack_min", [P, 1])
        tile_due = tmp("tile_due", [P, GROUPS + 3])
        zeros = tmp("zeros", [P, P], F16)
        iota_lo = tmp("iota_lo", [P, LO], F16)
        iota_hi = tmp("iota_hi", [P, HI], F16)
        deg_root = tmp("deg_root", [P, TILES])
        stats = tmp("stats", [P, TILES, 6])
        mean = tmp("mean", [P, TILES])
        var = tmp("var", [P, TILES])
        gap = tmp("gap", [P, TILES])

        s_edge = sem("edges_loaded")
        s_wt = sem("weights_loaded")
        s_weight = sem("edge_weights_loaded")
        s_moe = sem("expert_weights_loaded")
        s_x = sem("x_loaded")
        s_const = sem("constants_ready")
        s_extent = sem("extent_ready")
        s_extent_all = sem("extent_reduced")
        s_var = sem("variance_ready")
        s_std = sem("deviation_ready")
        s_chain_v = sem("vector_step")
        s_chain_g = sem("gpsimd_step")
        WEIGHTS = 4
        EXPERT_WEIGHTS = 5
        chain = [0]

        def dve_steps(dve, *instructions):
            for ins in instructions:
                chain[0] += 1
                ins.then_inc(s_chain_v, 1)
            dve.wait_ge(s_chain_v, chain[0])

        with nc.Block() as block:
            @block.sync
            def _(sp):
                sp.dma_start(dst_i[:], dst).then_inc(s_edge, 16)
                for i in range(PASSES):
                    t = slice(i * BATCH, (i + 1) * BATCH)
                    sp.dma_start(rows[:, t, :], x_tiles[:, t, :]).then_inc(s_x, 16)
                sp.dma_start(w_edge[:], weight).then_inc(s_weight, 16)
                sp.dma_start(moe_w1_sb[:], moe_w1.rearrange("e (k p) n -> p e k n", p=P)).then_inc(s_moe, 16)
                sp.dma_start(moe_w2_sb[:], moe_w2.rearrange("e (k p) n -> p e k n", p=P)).then_inc(s_moe, 16)

            @block.scalar
            def _(act):
                act.dma_start(w1_sb[:], gnn_w1.rearrange("(k p) n -> p k n", p=P)).then_inc(s_wt, 16)
                act.dma_start(b1_sb[:], gnn_b1.partition_broadcast(P)).then_inc(s_wt, 16)
                act.dma_start(w2_sb[:], gnn_w2.rearrange("(k p) n -> p k n", p=P)).then_inc(s_wt, 16)
                act.dma_start(b2_sb[:], gnn_b2.partition_broadcast(P)).then_inc(s_wt, 16)
                act.dma_start(router_sb[:], router.rearrange("(k p) n -> p k n", p=P)).then_inc(s_moe, 16)
                act.dma_start(moe_b1_sb[:], moe_b1).then_inc(s_moe, 16)
                act.dma_start(moe_b2_sb[:], moe_b2).then_inc(s_moe, 16)

            @block.gpsimd
            def _(pool):
                def iota_of(out, pattern, base=0, per_partition=0):
                    nc.gpsimd.iota(out, pattern=pattern, base=base, channel_multiplier=per_partition,
                                   allow_small_or_imprecise_dtypes=True).then_inc(s_const, 1)

                iota_of(tile_due[:], [[P, STEPS + 1], [0, GROUPS_PER_STEP]], base=-P)
                nc.gpsimd.memset(eps[:], EPS).then_inc(s_const, 1)
                iota_of(iota[:], [[1, P]])
                iota_of(iota_lo[:], [[1, LO]])
                iota_of(iota_hi[:], [[1, HI]])
                nc.gpsimd.memset(zeros[:], 0.0).then_inc(s_const, 1)
                nc.gpsimd.memset(ident[:], 0.0).then_inc(s_chain_g, 1)
                pool.wait_ge(s_chain_g, 1)
                nc.gpsimd.affine_select(out=ident[:], in_=ident[:], compare_op=ALU.not_equal, fill=1.0,
                                        base=0, pattern=[[-1, P]], channel_multiplier=1).then_inc(s_const, 1)
                pool.wait_ge(s_extent, 2)
                nc.gpsimd.partition_all_reduce(extent_all[:].rearrange("p a g -> p (a g)"),
                                               extent[:].rearrange("p a g -> p (a g)"), P, RMAX)\
                    .then_inc(s_extent_all, 1)

            @block.vector
            def _(dve):
                dve.wait_ge(s_edge, 16)
                dve_steps(dve, nc.vector.tensor_copy(dst_f[:], dst_i[:]))
                by_group = dst_f[:].rearrange("p (g c) -> p g c", c=GROUP)
                nc.vector.tensor_reduce(extent[:, 0, :], by_group, AX, ALU.min, negate=True).then_inc(s_extent, 1)
                nc.vector.tensor_reduce(extent[:, 1, :], by_group, AX, ALU.max).then_inc(s_extent, 1)

                dve.wait_ge(s_const, 7)
                dve.wait_ge(s_extent_all, 1)
                dve_steps(dve,
                          nc.vector.tensor_tensor(span[:], extent_all[:, 0, :], extent_all[:, 1, :], ALU.add),
                          nc.vector.tensor_scalar(base_f[:], extent_all[:, 0, :], -1.0, None, ALU.mult))
                dve_steps(dve,
                          nc.vector.tensor_reduce(span_max[:], span[:, 0:GROUPS], AX, ALU.max),
                          nc.vector.tensor_copy(base_i[:], base_f[:]),
                          nc.vector.tensor_tensor(slack[:], base_f[:], tile_due[:, 1:GROUPS + 2], ALU.subtract))
                dve_steps(dve,
                          nc.vector.tensor_copy(span_i[:], span_max[:]),
                          nc.vector.tensor_reduce(slack_min[:], slack[:, 0:GROUPS], AX, ALU.min))
                dve_steps(dve,
                          nc.vector.tensor_scalar(span_i[:], span_i[:], WINDOW.bit_length() - 1, None,
                                                  ALU.logical_shift_right),
                          nc.vector.tensor_scalar(slack_min[:], slack_min[:], 0.0, None, ALU.is_ge),
                          nc.vector.tensor_scalar(span_max[:], span_max[:], float(WINDOW), None, ALU.is_lt))
                dve_steps(dve,
                          nc.vector.tensor_scalar(choice_i[:, 0:1], span_i[:], 1.0, None, ALU.add),
                          nc.vector.tensor_tensor(choice_i[:, 1:2], slack_min[:], span_max[:], ALU.mult))

        def norm_factors_dve(dve):
            dve.wait_ge(s_x, PASSES * 16)
            with dve.Fori(0, PASSES) as it:
                for j in range(BATCH):
                    t = bass.ds(it * BATCH + j, 1)
                    nc.vector.bn_stats(stats[:, t, :].rearrange("p a b -> p (a b)"),
                                       rows[:, t, :].rearrange("p a b -> p (a b)")).then_inc(s_stats, 1)
            dve.wait_ge(s_stats, TILES)
            mean_even, squares_even, mean_odd, squares_odd = [stats[:, :, k] for k in (1, 2, 4, 5)]
            nc.vector.tensor_tensor(mean[:], mean_even, mean_odd, ALU.add).then_inc(s_factor, 1)
            nc.vector.tensor_tensor(gap[:], mean_even, mean_odd, ALU.subtract).then_inc(s_factor, 1)
            nc.vector.tensor_tensor(var[:], squares_even, squares_odd, ALU.add).then_inc(s_factor, 1)
            dve.wait_ge(s_factor, 3)
            nc.vector.tensor_tensor(gap[:], gap[:], gap[:], ALU.mult).then_inc(s_factor, 1)
            nc.vector.tensor_scalar(mean[:], mean[:], 0.5, None, ALU.mult).then_inc(s_factor, 1)
            nc.vector.tensor_scalar(var[:], var[:], 1.0 / D, None, ALU.mult).then_inc(s_factor, 1)
            dve.wait_ge(s_factor, 6)
            nc.vector.scalar_tensor_tensor(var[:], gap[:], 0.25, var[:], ALU.mult, ALU.add).then_inc(s_var, 1)
            dve.wait_ge(s_std, 1)
            nc.vector.reciprocal(rstd[:], rstd[:]).then_inc(s_factor, 1)
            dve.wait_ge(s_factor, 7)
            nc.vector.scalar_tensor_tensor(shift[:], mean[:], -1.0, rstd[:], ALU.mult, ALU.mult)\
                .then_inc(s_factor, 1)
            dve.wait_ge(s_factor, 8)

        def norm_deviation_act(act):
            act.wait_ge(s_var, 1)
            nc.scalar.activation(rstd[:], var[:], ACT.Sqrt, bias=eps[:, 0:1]).then_inc(s_std, 1)

        def scale_factors_dve(dve):
            dve.wait_ge(s_root, 1)
            nc.vector.reciprocal(dinv[:, 0:TILES], deg_root[:]).then_inc(s_factor, 1)
            dve.wait_ge(s_factor, 9)
            nc.vector.tensor_tensor(rstd[:], rstd[:], dinv[:, 0:TILES], ALU.mult)
            nc.vector.tensor_tensor(shift[:], shift[:], dinv[:, 0:TILES], ALU.mult)

        def padding_pool(pool):
            nc.gpsimd.memset(dinv[:, TILES:TILES_PAD], 1.0)

        s_stats = sem("row_statistics")
        s_factor = sem("factor_step")
        s_root = sem("degree_root")
        s_turn_pe = sem("turn_tensor")

        def degrees_of_windows(temporary):
            def tmp_(name, shape, dt):
                return tmp(name, shape, dt, temporary)

            LOWS = LOW * GROUP
            ROUND = PARTS_PER_ROUND * PART
            MADE = ROUND + ROUND % 2
            lo_h = tmp_("low_digit", [P, CHUNKS_PAD], F16)
            hi_h = tmp_("high_digit", [P, CHUNKS_PAD], F16)
            base_hi_i = tmp_("base_high_i", [P, GROUPS + 1], I32)
            base_hi = tmp_("base_high", [P, GROUPS + 1], F32)
            low_hot = tmp_("low_hot", [P, 2, MADE, LOW, GROUP], F16)
            high_hot = tmp_("high_hot", [P, 2, MADE, HIGHS, GROUP], F16)
            blocks = tmp_("count_blocks", [LOWS, GROUPS, BLOCK], F16)
            pick = tmp_("pick_chunk", [LOWS, LOWS], F16)
            shifted = tmp_("counts_padded", [P, 2, HIGHS, PAD + LOW + PAD], F16)
            base_col = tmp_("base_column", [P, 2], F32)
            high_of = tmp_("high_of", [P, HIGHS + HIGHS_OF_TILE - 1, TILES], F16)
            starts = tmp_("window_starts", [P, 2, HIGHS + HIGHS_OF_TILE - 1, TILES], F16)
            sets = [(0, P), (P, GROUPS)]

            s_step = sem("digits_step")
            s_fill = sem("count_constants")
            s_hot = sem("digit_onehots")
            s_hist = sem("chunks_counted")
            s_block = sem("blocks_copied")
            s_base_t = sem("base_transposed")
            s_base_c = sem("base_by_partition")
            s_start = sem("starts_ready")
            s_count = sem("groups_counted")
            s_shift = sem("counts_in_place")
            s_deg = sem("degree_even")

            ROUNDS = PARTS // PARTS_PER_ROUND

            with nc.Block() as block:
                @block.gpsimd
                def _(pool):
                    padding_pool(pool)
                    nc.gpsimd.tensor_tensor(dst_rel[:].rearrange("p (g c) -> p g c", c=GROUP),
                                            dst_f[:].rearrange("p (g c) -> p g c", c=GROUP),
                                            bc(base_f[:].unsqueeze(2), [P, GROUPS + 1, GROUP]), ALU.subtract)
                    nc.gpsimd.memset(shifted[:], 0.0).then_inc(s_fill, 1)
                    nc.gpsimd.iota(high_of[:], pattern=[[1, HIGHS + HIGHS_OF_TILE - 1], [HIGHS_OF_TILE, TILES]],
                                   base=1 - HIGHS, channel_multiplier=0,
                                   allow_small_or_imprecise_dtypes=True).then_inc(s_fill, 1)

                @block.vector
                def _(dve):
                    def step(k, *instructions):
                        for ins in instructions:
                            ins.then_inc(s_step, 1)
                        dve.wait_ge(s_step, k)

                    step(2, nc.vector.tensor_scalar(base_hi_i[:], base_i[:], LOW.bit_length() - 1, None,
                                                    ALU.logical_shift_right),
                         nc.vector.tensor_scalar(dst_i[:], dst_i[:], LOW.bit_length() - 1, None,
                                                 ALU.logical_shift_right))
                    step(3, nc.vector.tensor_copy(base_hi[:], base_hi_i[:]))
                    step(6, nc.vector.scalar_tensor_tensor(lo_h[:], dst_i[:], -float(LOW), dst_f[:], ALU.mult,
                                                           ALU.add),
                         nc.vector.tensor_tensor(hi_h[:].rearrange("p (g c) -> p g c", c=GROUP),
                                                 dst_i[:].rearrange("p (g c) -> p g c", c=GROUP),
                                                 bc(base_hi[:].unsqueeze(2), [P, GROUPS + 1, GROUP]),
                                                 ALU.subtract),
                         nc.vector.tensor_copy(pick[:], ident[0:LOWS, 0:LOWS]))

                    for rnd in range(ROUNDS):
                        if rnd >= 2:
                            dve.wait_ge(s_hist, (rnd - 1) * PARTS_PER_ROUND)
                        chunks = slice(rnd * ROUND * GROUP, (rnd * ROUND + MADE) * GROUP)
                        for hot, digit, size in ((low_hot, lo_h, LOW), (high_hot, hi_h, HIGHS)):
                            for k in range(size):
                                nc.vector.tensor_scalar(hot[:, rnd % 2, :, k, :],
                                                        digit[:, chunks].rearrange("p (g c) -> p g c", c=GROUP),
                                                        float(k), None, ALU.is_equal).then_inc(s_hot, 1)
                    dve.wait_ge(s_base_t, 1)
                    for k, (first, last) in enumerate(sets):
                        nc.vector.tensor_copy(base_col[0:last - first, k:k + 1],
                                              bank[7][0:last - first, P * (k + 1):P * (k + 1) + 1])\
                            .then_inc(s_base_c, 1)
                    dve.wait_ge(s_base_c, 2)
                    dve.wait_ge(s_fill, 2)
                    for k, (first, last) in enumerate(sets):
                        nc.vector.tensor_scalar(starts[0:last - first, k], high_of[0:last - first],
                                                base_col[0:last - first, k:k + 1], None, ALU.is_equal)\
                            .then_inc(s_start, 1)
                    norm_factors_dve(dve)
                    scale_factors_dve(dve)

                @block.scalar
                def _(act):
                    for part in range(PARTS):
                        act.wait_ge(s_hist, part + 1)
                        for b, first in enumerate(range(0, PART, COUNTED_TOGETHER)):
                            number = min(COUNTED_TOGETHER, PART - first)
                            group = part * PART + first
                            nc.scalar.activation(blocks[:, group:group + number, :],
                                                 bank[2 * (part % PARTS_PER_ROUND) + b][0:LOWS, 0:number * BLOCK]
                                                 .rearrange("p (g n) -> p g n", n=BLOCK), ACT.Copy)\
                                .then_inc(s_block, 1)
                    act.wait_ge(s_count, 1)
                    act.wait_ge(s_fill, 2)
                    for k, (first, last) in enumerate(sets):
                        nc.scalar.activation(shifted[0:last - first, k, :, PAD:PAD + LOW],
                                             bank[6 + k][0:last - first, 0:HIGHS * LOW]
                                             .rearrange("p (h l) -> p h l", l=LOW), ACT.Copy).then_inc(s_shift, 1)
                    norm_deviation_act(act)
                    act.wait_ge(s_deg, 1)
                    nc.scalar.activation(deg_root[:], bank[0][:, 0:TILES], ACT.Sqrt, bias=1.0).then_inc(s_root, 1)

                @block.tensor
                def _(pe):
                    pe.wait_ge(s_step, 3)
                    for k, (first, last) in enumerate(sets):
                        ins = nc.tensor.transpose(bank[7][0:last - first, P * (k + 1):P * (k + 2)],
                                                  base_hi[:, first:last], ident[:])
                    ins.then_inc(s_base_t, 1)
                    for part in range(PARTS):
                        rnd, j = divmod(part, PARTS_PER_ROUND)
                        pe.wait_ge(s_hot, (rnd + 1) * (LOW + HIGHS))
                        if part >= PARTS_PER_ROUND:
                            pe.wait_ge(s_block, 2 * (part - PARTS_PER_ROUND + 1))
                        for g in range(PART):
                            group = j * PART + g
                            b, at = divmod(g, COUNTED_TOGETHER)
                            ins = nc.tensor.matmul(
                                bank[2 * j + b][0:LOWS, at * BLOCK:(at + 1) * BLOCK],
                                low_hot[:, rnd % 2, group].rearrange("p n c -> p (n c)"),
                                high_hot[:, rnd % 2, group].rearrange("p n c -> p (n c)"),
                                start=True, stop=True)
                        ins.then_inc(s_hist, 1)
                    pe.wait_ge(s_block, 2 * PARTS)
                    pe.wait_ge(s_base_c, 2)
                    for h in range(HIGHS):
                        for k, (first, last) in enumerate(sets):
                            for c in range(GROUP):
                                nc.tensor.matmul(bank[6 + k][0:last - first, h * LOW:(h + 1) * LOW],
                                                 blocks[:, first:last, h * GROUP + c], pick[:, c::GROUP],
                                                 start=(c == 0), stop=(c == GROUP - 1))
                    nc.tensor.matmul(bank[0][:, 0:TILES], zeros[:], zeros[:, 0:TILES], start=True, stop=False)\
                        .then_inc(s_count, 1)
                    pe.wait_ge(s_shift, 2)
                    pe.wait_ge(s_start, 2)
                    for h in range(HIGHS):
                        for q in range(HIGHS_OF_TILE):
                            for k, (first, last) in enumerate(sets):
                                at = PAD - q * LOW
                                nc.tensor.matmul(bank[0][:, 0:TILES], shifted[0:last - first, k, h, at:at + P],
                                                 starts[0:last - first, k, q + HIGHS - 1 - h, :],
                                                 start=False, stop=False)
                    nc.tensor.matmul(bank[0][:, 0:TILES], zeros[:], zeros[:, 0:TILES], start=False, stop=True)\
                        .then_inc(s_deg, 1)

        def degrees_of_edges(temporary):
            def tmp_(name, shape, dt):
                return tmp(name, shape, dt, temporary)

            lo_i = tmp_("lo_i", [P, CHUNKS_PAD], I32)
            lo_b = tmp_("lo_b", [P, CHUNKS_PAD], F16)
            hi_b = tmp_("hi_b", [P, CHUNKS_PAD], F16)
            onehot_lo = tmp_("onehot_lo", [P, GROUPS_PER_STEP, GROUP, LO], F16)
            onehot_hi = tmp_("onehot_hi", [P, GROUPS_PER_STEP, GROUP, HI], F16)
            deg_lohi = tmp_("deg_lohi", [LO, TILES, 2], F32)
            deg = tmp_("deg", [P, TILES], F32)
            s_split = sem("dst_split_any")
            s_hot = sem("onehots_any")
            s_used = sem("onehots_used_any")
            s_deg = sem("degree_any")
            s_deg_sb = sem("degree_copied")
            s_deg_tile = sem("degree_by_tile")
            with nc.Block() as block:
                @block.sync
                def _(sp):
                    sp.wait_ge(s_deg_sb, 1)
                    for odd in range(2):
                        with nc.allow_non_contiguous_dma(reason="49 degrees per partition"):
                            sp.dma_start(deg[odd * LO:(odd + 1) * LO, :], deg_lohi[:, :, odd])\
                                .then_inc(s_deg_tile, 16)

                @block.gpsimd
                def _(pool):
                    padding_pool(pool)

                @block.scalar
                def _(act):
                    norm_deviation_act(act)
                    act.wait_ge(s_deg_tile, 32)
                    nc.scalar.activation(deg_root[:], deg[:], ACT.Sqrt, bias=1.0).then_inc(s_root, 1)

                @block.vector
                def _(dve):
                    def split(k, ins):
                        ins.then_inc(s_split, 1)
                        dve.wait_ge(s_split, k)
                    norm_factors_dve(dve)
                    split(1, nc.vector.tensor_scalar(lo_i[:], dst_i[:], LO - 1, None, ALU.bitwise_and))
                    split(2, nc.vector.tensor_copy(lo_b[:], lo_i[:]))
                    split(3, nc.vector.tensor_scalar(lo_i[:], dst_i[:], LO.bit_length() - 1, None,
                                                     ALU.logical_shift_right))
                    split(4, nc.vector.tensor_copy(hi_b[:], lo_i[:]))
                    with dve.Fori(0, STEPS) as it:
                        for j in range(GROUPS_PER_STEP):
                            dve.wait_ge(s_used, it * GROUPS_PER_STEP + j + 1)
                            c = bass.ds(it * CHUNKS_PER_STEP + j * GROUP, GROUP)
                            nc.vector.tensor_tensor(
                                onehot_lo[:, j], bc(iota_lo[:].unsqueeze(1), [P, GROUP, LO]),
                                bc(lo_b[:, c].unsqueeze(2), [P, GROUP, LO]), ALU.is_equal).then_inc(s_hot, 1)
                            nc.vector.tensor_tensor(
                                onehot_hi[:, j], bc(iota_hi[:].unsqueeze(1), [P, GROUP, HI]),
                                bc(hi_b[:, c].unsqueeze(2), [P, GROUP, HI]), ALU.is_equal).then_inc(s_hot, 1)
                    dve.wait_ge(s_deg, 1)
                    nc.vector.tensor_copy(deg_lohi[:], bank[3][0:LO, 0:HI].rearrange("p (t o) -> p t o", o=2))\
                        .then_inc(s_deg_sb, 1)
                    scale_factors_dve(dve)

                @block.tensor
                def _(pe):
                    pe.sem_inc(s_used, GROUPS_PER_STEP)
                    nc.tensor.matmul(bank[3][0:LO, 0:HI], zeros[:, 0:LO], zeros[:, 0:HI], start=True, stop=False)
                    with pe.Fori(0, STEPS) as it:
                        for j in range(GROUPS_PER_STEP):
                            pe.wait_ge(s_hot, (it * GROUPS_PER_STEP + j) * 2 + 2)
                            for c in range(GROUP):
                                last = nc.tensor.matmul(bank[3][0:LO, 0:HI], onehot_lo[:, j, c], onehot_hi[:, j, c],
                                                        start=False, stop=False)
                            last.then_inc(s_used, 1)
                    nc.tensor.matmul(bank[3][0:LO, 0:HI], zeros[:, 0:LO], zeros[:, 0:HI], start=False, stop=True)\
                        .then_inc(s_deg, 1)

        rounds = nc.values_load(choice_i[0:1, 0:1], min_val=1, max_val=NODES // WINDOW + 1)
        spread = nc.values_load(choice_i[0:1, 1:2], min_val=0, max_val=1)
        with nc.If(spread == 1):
            with ExitStack() as temporary:
                degrees_of_windows(temporary)
        with nc.Else():
            with ExitStack() as temporary:
                degrees_of_edges(temporary)

        setup_ctx.close()
        agg = sb("agg", [P, HALF, AGG])
        place = sb("place", [P, GROUPS_PER_STEP, GROUP, WINDOW])
        sum_rows = sb("sum_rows", [WINDOW, D])
        small = sb("small", [P, 66])
        top_u = sb("top_u", [P, 8], mybir.dt.uint32)
        comb_t = sb("comb_t", [EXPERTS, P])

        def write_first_table():
            s_xn = sem("normalised_rows")
            s_t = sem("rows_transposed")
            s_xt = sem("transposed_copied")
            s_h = sem("row_product")
            s_g = sem("table_rows")
            s_store = sem("table_stored")
            row = lambda t: rows[:, bass.ds(t, 1), :].rearrange("p a b -> p (a b)")

            with nc.Block() as block:
                @block.sync
                def _(sp):
                    with sp.Fori(0, PASSES) as it:
                        tiles = bass.ds(it * BATCH, BATCH)
                        sp.wait_ge(s_g, it * BATCH + (BATCH + 2))
                        sp.dma_start(table_1_tiles[:, tiles, :], rows[:, tiles, :]).then_inc(s_store, 16)
                    sp.wait_ge(s_store, PASSES * 16)

                @block.gpsimd
                def _(pool):
                    nc.gpsimd.memset(agg[:], 0.0)

                @block.scalar
                def _(act):
                    def normalise(t, j):
                        nc.scalar.activation(buf_a[:, j, :], row(t), ACT.Identity, scale=rstd[:, bass.ds(t, 1)],
                                             bias=shift[:, bass.ds(t, 1)]).then_inc(s_xn, 1)

                    with act.Fori(0, PASSES) as it:
                        normalise(it * BATCH, 0)
                        for j in range(BATCH):
                            t = it * BATCH + j
                            if j + 1 < BATCH:
                                normalise(t + 1, j + 1)
                            act.wait_ge(s_t, t + 1)
                            nc.scalar.activation(buf_b[:, j, :], bank[1 + j % 2][:, 0:D], ACT.Copy).then_inc(s_xt, 1)

                @block.tensor
                def _(pe):
                    def transpose(t, j):
                        pe.wait_ge(s_xn, t + 1)
                        pe.wait_ge(s_xt, t + (1 if j else 2))
                        pe.sem_inc(s_turn_pe, 1)
                        for k in range(HALF):
                            last = nc.tensor.transpose(bank[1 + j % 2][:, k * P:(k + 1) * P],
                                                       buf_a[:, j, k * P:(k + 1) * P], ident[:])
                        last.then_inc(s_t, 1)

                    pe.wait_ge(s_wt, 16 * WEIGHTS)
                    pe.sem_inc(s_xt, 2)
                    pe.sem_inc(s_g, 2)
                    with pe.Fori(0, PASSES) as it:
                        transpose(it * BATCH, 0)
                        for j in range(BATCH):
                            t = it * BATCH + j
                            if j + 1 < BATCH:
                                transpose(t + 1, j + 1)
                            pe.wait_ge(s_xt, t + 3)
                            pe.wait_ge(s_g, t + (1 if j else 2))
                            for k in range(HALF):
                                last = nc.tensor.matmul(bank[3 + j % 2][:, 0:D], buf_b[:, j, k * P:(k + 1) * P],
                                                        w1_sb[:, k, :], start=(k == 0), stop=(k == HALF - 1))
                            last.then_inc(s_h, 1)

                @block.vector
                def _(dve):
                    with dve.Fori(0, PASSES) as it:
                        for j in range(BATCH):
                            t = it * BATCH + j
                            dve.wait_ge(s_h, t + 1)
                            nc.vector.scalar_tensor_tensor(row(t), b1_sb[:], dinv[:, bass.ds(t, 1)],
                                                           bank[3 + j % 2][:, 0:D], ALU.mult, ALU.add)\
                                .then_inc(s_g, 1)

        def windows(tag):
            s_window = sem(f"windows_{tag}")

            def make(dve):
                nc.vector.tensor_copy(base_i[:], base_f[:]).then_inc(s_window, 1)
                nc.vector.tensor_tensor(dst_rel[:].rearrange("p (g c) -> p g c", c=GROUP),
                                        dst_f[:].rearrange("p (g c) -> p g c", c=GROUP),
                                        bc(base_f[:].unsqueeze(2), [P, GROUPS + 1, GROUP]),
                                        ALU.subtract).then_inc(s_window, 1)
                dve.wait_ge(s_window, 2)
            return make

        def edge_sums(tag, table, layer):
            s_idx = [sem(f"indices_{tag}{j}") for j in range(GROUPS_PER_STEP)]
            s_row = [sem(f"rows_gathered_{tag}{j}") for j in range(GROUPS_PER_STEP)]
            s_last = [sem(f"last_rows_gathered_{tag}{j}") for j in range(GROUPS_PER_STEP)]
            s_eq = sem(f"edge_columns_{tag}")
            s_place = sem(f"placed_{tag}")
            s_sum = sem(f"group_summed_{tag}")
            s_copy = sem(f"sums_copied_{tag}")
            s_t = sem(f"sums_transposed_{tag}")
            s_add = sem(f"sums_added_{tag}")
            s_turn = sem(f"turn_{tag}")

            def sp_indices(sp, it, j, n):
                sp.wait_ge(s_sum, n + 1)
                sp.dma_start(idx[:, layer, j, :], src[:, bass.ds(it * CHUNKS_PER_STEP + j * GROUP, GROUP)])\
                    .then_inc(s_idx[j], 16)

            def sp_first_indices(sp, j):
                sp.dma_start(idx[:, layer, j, :], src[:, j * GROUP:(j + 1) * GROUP]).then_inc(s_idx[j], 16)

            def pool_gather(pool, j, step):
                pool.wait_ge(s_idx[j], step * 16 + 16)
                pool.sem_inc(s_turn, 1)
                for c in range(GROUP):
                    nc.gpsimd.indirect_dma_start(ring[:, j * GROUP + c, :], None, table,
                                                 bass.IndirectOffsetOnAxis(ap=idx[:, layer, j, c:c + 1], axis=0))\
                        .then_inc(s_row[j] if c < EARLY else s_last[j], 16)

            def dve_place(dve, it, j, n):
                c = it * CHUNKS_PER_STEP + j * GROUP
                slot = place[:, j % GROUPS_PER_STEP]
                dve.wait_ge(s_sum, n + 1)
                nc.vector.tensor_tensor(slot, bc(iota[:, 0:WINDOW].unsqueeze(1), [P, GROUP, WINDOW]),
                                        bc(dst_rel[:, bass.ds(c, GROUP)].unsqueeze(2), [P, GROUP, WINDOW]),
                                        ALU.is_equal).then_inc(s_eq, 1)
                dve.wait_ge(s_eq, n + 1)
                nc.vector.tensor_tensor(slot, slot, bc(w_edge[:, bass.ds(c, GROUP)].unsqueeze(2),
                                                       [P, GROUP, WINDOW]), ALU.mult).then_inc(s_place, 1)

            def dve_add(dve, it, j, n):
                first = dve.value_load(base_i[0:1, bass.ds(it * GROUPS_PER_STEP + j, 1)], min_val=0, max_val=NODES)
                dve.wait_ge(s_t, n + 1)
                dve.wait_ge(s_add, n + 1)
                window = agg[:, :, bass.ds(first, WINDOW)]
                nc.vector.tensor_tensor(window, window, bank[1][:, 0:HALF * WINDOW]
                                        .rearrange("p (k n) -> p k n", k=HALF), ALU.add).then_inc(s_add, 1)

            def act_copy(act, n):
                act.wait_ge(s_sum, n + 1 + GROUPS_PER_STEP)
                nc.scalar.activation(sum_rows[:], bank[0][0:WINDOW, 0:D], ACT.Copy).then_inc(s_copy, 1)

            def pe_sum(pe, it, j, n):
                pe.wait_ge(s_place, n + 1)
                pe.wait_ge(s_row[j], it * (16 * EARLY) + 16 * EARLY)
                for c in range(GROUP):
                    if c == EARLY:
                        pe.wait_ge(s_last[j], it * (16 * (GROUP - EARLY)) + 16 * (GROUP - EARLY))
                    last = nc.tensor.matmul(bank[0][0:WINDOW, 0:D], place[:, j, c], ring[:, j * GROUP + c, :],
                                            start=(c == 0), stop=(c == GROUP - 1))
                last.then_inc(s_sum, 1)

            def pe_transpose(pe, n):
                pe.wait_ge(s_copy, n + 1)
                pe.wait_ge(s_add, n + 1)
                pe.sem_inc(s_turn, 1)
                for k in range(HALF):
                    last = nc.tensor.transpose(bank[1][:, k * WINDOW:(k + 1) * WINDOW],
                                               sum_rows[:, k * P:(k + 1) * P], ident[0:WINDOW, 0:WINDOW])
                last.then_inc(s_t, 1)

            def wait_added(eng, n):
                eng.wait_ge(s_add, n + 2)

            parts = Parts()
            parts.sp_indices = sp_indices
            parts.sp_first_indices = sp_first_indices
            parts.pool_gather = pool_gather
            parts.dve_place = dve_place
            parts.dve_add = dve_add
            parts.act_copy = act_copy
            parts.pe_sum = pe_sum
            parts.pe_transpose = pe_transpose
            parts.wait_added = wait_added
            parts.s_add = s_add
            parts.s_row = s_row
            parts.s_last = s_last
            parts.s_sum = s_sum
            parts.s_turn = s_turn
            return parts

        def sum_edges_in_rounds(tag, table, layer, rounds):
            make_windows = windows(tag)
            e = edge_sums(tag, table, layer)
            s_next = sem(f"next_round_{tag}")
            with nc.Block() as block:
                @block.vector
                def _(dve):
                    make_windows(dve)
                    dve.wait_ge(s_weight, 16)
                    dve.sem_inc(e.s_add, 1)

                @block.tensor
                def _(pe):
                    pe.sem_inc(e.s_sum, GROUPS_PER_STEP)

            with nc.Fori(0, rounds) as rnd:
                with nc.Block() as block:
                    def steps(eng):
                        with eng.Fori(0, STEPS) as it:
                            for j in range(GROUPS_PER_STEP):
                                step = rnd * STEPS + it
                                yield it, j, step, step * GROUPS_PER_STEP + j

                    @block.sync
                    def _(sp):
                        for it, j, step, n in steps(sp):
                            e.sp_indices(sp, it, j, n)

                    @block.gpsimd
                    def _(pool):
                        for it, j, step, n in steps(pool):
                            e.pool_gather(pool, j, step)

                    @block.vector
                    def _(dve):
                        for it, j, step, n in steps(dve):
                            e.dve_place(dve, it, j, n)
                            e.dve_add(dve, it, j, n)
                        nc.vector.tensor_scalar(base_i[:], base_i[:], float(WINDOW), float(NODES), ALU.add,
                                                ALU.min).then_inc(s_next, 1)
                        nc.vector.tensor_scalar(dst_rel[:], dst_rel[:], -float(WINDOW), None, ALU.add)\
                            .then_inc(s_next, 1)
                        dve.wait_ge(s_next, rnd * 2 + 2)
                        dve.sem_inc(e.s_turn, 1)

                    @block.scalar
                    def _(act):
                        for it, j, step, n in steps(act):
                            e.act_copy(act, n)

                    @block.tensor
                    def _(pe):
                        for it, j, step, n in steps(pe):
                            e.pe_sum(pe, it, j, n)
                            e.pe_transpose(pe, n)

                with nc.Block() as block:
                    @block.gpsimd
                    def _(pool):
                        pool.dma_reset()
                        for j in range(GROUPS_PER_STEP):
                            pool.sem_clear(e.s_row[j])
                            pool.sem_clear(e.s_last[j])

        def second_table():
            relu_t, biased, table_row, own_row, summed = [buf_a[:, i, :] for i in range(5)]
            s_own = sem("mid_own_loaded")
            s_turn_dve = sem("turn_vector")
            s_own_t = sem("mid_own_transposed")
            s_summed = sem("mid_own_added")
            s_relu = sem("mid_relu")
            s_u = sem("mid_product")
            s_v = sem("mid_biased")
            s_g = sem("mid_rows")
            s_gt = sem("mid_transposed")
            s_loop = sem("mid_self_loops")
            s_store = sem("mid_store")

            def sp_own(sp, m, first=False):
                if not first:
                    sp.wait_ge(s_own_t, m)
                sp.dma_start(own_row, table_1[bass.ds(m * P, P), :]).then_inc(s_own, 16)

            def pe_own(pe, m):
                pe.wait_ge(s_own, m * 16 + 16)
                for k in range(HALF):
                    last = nc.tensor.transpose(bank[4][:, k * P:(k + 1) * P], own_row[:, k * P:(k + 1) * P],
                                               ident[:])
                last.then_inc(s_own_t, 1)

            def dve_own(dve, m):
                dve.wait_ge(s_own_t, m + 1)
                nc.vector.tensor_tensor(summed.rearrange("p (k n) -> p k n", k=HALF),
                                        bank[4][:, 0:D].rearrange("p (k n) -> p k n", k=HALF),
                                        agg[:, :, bass.ds(m * P, P)], ALU.add).then_inc(s_summed, 1)

            def act_relu(act, m):
                act.wait_ge(s_summed, m + 1)
                nc.scalar.activation(relu_t, summed, ACT.Relu).then_inc(s_relu, 1)

            def pe_product(pe, m):
                pe.wait_ge(s_relu, m + 1)
                for k in range(HALF):
                    last = nc.tensor.matmul(bank[2][:, 0:D], relu_t[:, k * P:(k + 1) * P], w2_sb[:, k, :],
                                            start=(k == 0), stop=(k == HALF - 1))
                last.then_inc(s_u, 1)

            def dve_bias(dve, m):
                dve.wait_ge(s_u, m + 1)
                nc.vector.scalar_tensor_tensor(biased, bank[2][:, 0:D], dinv[:, bass.ds(m, 1)], b2_sb[:],
                                               ALU.mult, ALU.add).then_inc(s_v, 1)

            def act_row(act, m):
                act.wait_ge(s_v, m + 1)
                nc.scalar.activation(table_row, biased, ACT.Copy, scale=dinv[:, bass.ds(m, 1)]).then_inc(s_g, 1)
                act.wait_ge(s_g, m + 1)
                act.dma_start(table_2[bass.ds(m * P, P), :], table_row).then_inc(s_store, 16)

            def act_stored(act, m):
                act.wait_ge(s_store, m * 16 + 16)
                act.wait_ge(s_gt, m + 1)

            def pe_transpose(pe, m):
                pe.wait_ge(s_g, m + 1)
                for k in range(HALF):
                    last = nc.tensor.transpose(bank[3][:, k * P:(k + 1) * P], table_row[:, k * P:(k + 1) * P],
                                               ident[:])
                last.then_inc(s_gt, 1)

            def dve_self_loops(dve, m):
                dve.wait_ge(s_gt, m + 1)
                dve.sem_inc(s_turn_dve, 1)
                nc.vector.tensor_copy(agg[:, :, bass.ds(m * P, P)],
                                      bank[3][:, 0:D].rearrange("p (k n) -> p k n", k=HALF)).then_inc(s_loop, 1)

            def pe_self_loops_done(pe, m):
                pe.wait_ge(s_loop, m + 1)

            parts = Parts()
            parts.sp_own = sp_own
            parts.pe_own = pe_own
            parts.dve_own = dve_own
            parts.act_relu = act_relu
            parts.pe_product = pe_product
            parts.dve_bias = dve_bias
            parts.act_row = act_row
            parts.act_stored = act_stored
            parts.pe_transpose = pe_transpose
            parts.dve_self_loops = dve_self_loops
            parts.pe_self_loops_done = pe_self_loops_done
            return parts

        def expert_tiles():
            x_in, x1, y, x1_y, y_t, total, relu_t = [buf_a[:, i, :] for i in range(7)]
            hidden = [buf_b[:, i, :] for i in range(2)]
            rows_p, y_t_p = bank[2][:, 0:D], bank[2][:, D:2 * D]
            logits_p, comb_t_p, bias_p = bank[3][:, 0:EXPERTS], bank[3][0:EXPERTS, P:2 * P], bank[3][:, D:2 * D]
            hidden_p = [bank[4][:, 0:D], bank[5][:, 0:D]]
            expert_p = [bank[6][:, 0:D], bank[7][:, 0:D]]
            mstat, mv = small[:, 0:6], small[:, 6:8]
            inv_std, neg_mean = small[:, 8:9], small[:, 9:10]
            neg_max, exp_sum, exp_inv = small[:, 10:11], small[:, 11:12], small[:, 12:13]
            pair_sum, pair_inv, top_w = small[:, 13:14], small[:, 14:15], small[:, 16:18]
            top_i, prob, top_p = small[:, 18:26], small[:, 26:34], small[:, 34:42]
            comb_0, comb_1, comb = small[:, 42:50], small[:, 50:58], small[:, 58:66]

            s_x = sem("tile_loaded")
            s_relu = sem("tile_relu")
            s_rows = sem("tile_rows")
            s_x1 = sem("tile_residual")
            s_var = sem("tile_variance")
            s_std = sem("tile_deviation")
            s_y = sem("tile_normalised")
            s_yt = sem("tile_transposed")
            s_yt_sb = sem("tile_transposed_copied")
            s_logit = sem("logits")
            s_nmax = sem("logit_max")
            s_exp = sem("logit_exp")
            s_comb = sem("combine_ready")
            s_comb_t = sem("combine_transposed")
            s_comb_sb = sem("combine_copied")
            s_bias = sem("combined_bias")
            s_hid = sem("hidden_product")
            s_gelu = sem("hidden_ready")
            s_exp_y = sem("expert_product")
            s_acc = sem("expert_added")
            s_store = sem("tile_store")
            s_chain = sem("expert_vector_step")
            chain = [0]

            def chain_restart(dve):
                dve.sem_clear(s_chain)
                chain[0] = 0

            def step(dve, ins):
                chain[0] += 1
                ins.then_inc(s_chain, 1)
                dve.wait_ge(s_chain, chain[0])

            def credits(pe):
                pe.wait_ge(s_moe, 16 * EXPERT_WEIGHTS)
                pe.sem_inc(s_hid, 1)
                pe.sem_inc(s_exp_y, 2)
                pe.sem_inc(s_acc, 2)

            def sp_load(sp, m, first=False):
                if not first:
                    sp.wait_ge(s_x1, m)
                sp.dma_start(x_in, x[bass.ds(m * P, P), :]).then_inc(s_x, 16)

            def act_relu(act, m, first=False):
                if not first:
                    act.wait_ge(s_rows, m)
                nc.scalar.activation(relu_t.rearrange("p (k n) -> p k n", k=HALF),
                                     agg[:, :, bass.ds(m * P, P)], ACT.Relu).then_inc(s_relu, 1)

            def pe_rows(pe, m):
                pe.wait_ge(s_relu, m + 1)
                for k in range(HALF):
                    last = nc.tensor.transpose(rows_p[:, k * P:(k + 1) * P], relu_t[:, k * P:(k + 1) * P], ident[:])
                last.then_inc(s_rows, 1)

            def dve_residual(dve, m):
                dve.wait_ge(s_rows, m + 1)
                dve.wait_ge(s_x, m * 16 + 16)
                nc.vector.scalar_tensor_tensor(x1, rows_p, dinv[:, bass.ds(m, 1)], x_in, ALU.mult,
                                               ALU.add).then_inc(s_x1, 1)
                dve.wait_ge(s_x1, m + 1)
                step(dve, nc.vector.bn_stats(mstat, x1))
                nc.vector.bn_aggr(mv, mstat).then_inc(s_var, 1)

            def act_std(act, m):
                act.wait_ge(s_var, m + 1)
                nc.scalar.activation(inv_std, mv[:, 1:2], ACT.Sqrt, bias=eps[:, 0:1]).then_inc(s_std, 1)

            def dve_normalise(dve, m, first=False):
                dve.wait_ge(s_std, m + 1)
                step(dve, nc.vector.reciprocal(inv_std, inv_std))
                step(dve, nc.vector.scalar_tensor_tensor(neg_mean, mv[:, 0:1], -1.0, inv_std, ALU.mult, ALU.mult))
                if not first:
                    dve.wait_ge(s_yt, m)
                nc.vector.tensor_scalar(y, x1, inv_std, neg_mean, ALU.mult, ALU.add).then_inc(s_y, 1)
                dve.wait_ge(s_y, m + 1)
                step(dve, nc.vector.tensor_tensor(x1_y, x1, y, ALU.add))

            def pe_y(pe, m, first=False):
                pe.wait_ge(s_y, m + 1)
                if not first:
                    pe.wait_ge(s_yt_sb, m)
                for k in range(HALF):
                    last = nc.tensor.transpose(y_t_p[:, k * P:(k + 1) * P], y[:, k * P:(k + 1) * P], ident[:])
                last.then_inc(s_yt, 1)

            def act_y_t(act, t):
                act.wait_ge(s_yt, t + 1)
                act.wait_ge(s_hid, t * EXPERTS + 1)
                nc.scalar.activation(y_t, y_t_p, ACT.Copy).then_inc(s_yt_sb, 1)

            def pe_logits(pe, t):
                pe.wait_ge(s_yt_sb, t + 1)
                for k in range(HALF):
                    last = nc.tensor.matmul(logits_p, y_t[:, k * P:(k + 1) * P], router_sb[:, k, :],
                                            start=(k == 0), stop=(k == 1))
                last.then_inc(s_logit, 1)

            def dve_logit_max(dve, t):
                dve.wait_ge(s_logit, t + 1)
                nc.vector.tensor_reduce(neg_max, logits_p, AX, ALU.max, negate=True).then_inc(s_nmax, 1)

            def act_exp(act, t):
                act.wait_ge(s_nmax, t + 1)
                nc.scalar.activation(prob, logits_p, ACT.Exp, bias=neg_max, accum_out=exp_sum).then_inc(s_exp, 1)

            def dve_combine(dve, t):
                dve.wait_ge(s_exp, t + 1)
                step(dve, nc.vector.reciprocal(exp_inv, exp_sum))
                step(dve, nc.vector.tensor_scalar(prob, prob, exp_inv, None, ALU.mult))
                step(dve, nc.vector.max(top_p, prob))
                step(dve, nc.vector.max_index(top_u[:], top_p, prob))
                step(dve, nc.vector.tensor_copy(top_i, top_u[:]))
                step(dve, nc.vector.tensor_tensor(pair_sum, top_p[:, 0:1], top_p[:, 1:2], ALU.add))
                step(dve, nc.vector.tensor_scalar(pair_sum, pair_sum, 1e-12, None, ALU.max))
                step(dve, nc.vector.reciprocal(pair_inv, pair_sum))
                step(dve, nc.vector.tensor_scalar(top_w, top_p[:, 0:2], pair_inv, None, ALU.mult))
                step(dve, nc.vector.tensor_scalar(comb_0, iota[:, 0:EXPERTS], top_i[:, 0:1], top_w[:, 0:1],
                                                  ALU.is_equal, ALU.mult))
                step(dve, nc.vector.tensor_scalar(comb_1, iota[:, 0:EXPERTS], top_i[:, 1:2], top_w[:, 1:2],
                                                  ALU.is_equal, ALU.mult))
                nc.vector.tensor_tensor(comb, comb_0, comb_1, ALU.add).then_inc(s_comb, 1)

            def pe_combine_t(pe, t):
                pe.wait_ge(s_comb, t + 1)
                nc.tensor.transpose(comb_t_p, comb, ident[:]).then_inc(s_comb_t, 1)

            def act_combine_t(act, t):
                act.wait_ge(s_comb_t, t + 1)
                nc.scalar.activation(comb_t[:], comb_t_p, ACT.Copy).then_inc(s_comb_sb, 1)

            def pe_bias(pe, t):
                pe.wait_ge(s_comb_sb, t + 1)
                nc.tensor.matmul(bias_p, comb_t[:], moe_b2_sb[:], start=True, stop=True).then_inc(s_bias, 1)

            def dve_total(dve, t, first=False):
                if not first:
                    dve.wait_ge(s_store, t * 16)
                dve.wait_ge(s_bias, t + 1)
                step(dve, nc.vector.tensor_tensor(total, bias_p, x1_y, ALU.add))

            def pe_hidden(pe, t, e):
                for f in range(HALF):
                    for k in range(HALF):
                        last = nc.tensor.matmul(hidden_p[e % 2][:, f * P:(f + 1) * P],
                                                moe_w1_sb[:, e, k, f * P:(f + 1) * P],
                                                y_t[:, k * P:(k + 1) * P], start=(k == 0), stop=(k == 1))
                last.then_inc(s_hid, 1)

            def act_gelu(act, t, e):
                act.wait_ge(s_hid, t * EXPERTS + e + 2)
                act.wait_ge(s_exp_y, t * EXPERTS + e + 1)
                for k in range(HALF):
                    nc.scalar.activation(hidden[e % 2][:, k * P:(k + 1) * P],
                                         hidden_p[e % 2][:, k * P:(k + 1) * P], ACT.Gelu,
                                         bias=moe_b1_sb[:, e * HALF + k:e * HALF + k + 1]).then_inc(s_gelu, 1)

            def pe_expert(pe, t, e):
                pe.wait_ge(s_gelu, (t * EXPERTS + e) * HALF + HALF)
                pe.wait_ge(s_acc, t * EXPERTS + e + 1)
                for f in range(HALF):
                    last = nc.tensor.matmul(expert_p[e % 2], hidden[e % 2][:, f * P:(f + 1) * P],
                                            moe_w2_sb[:, e, f, :], start=(f == 0), stop=(f == 1))
                last.then_inc(s_exp_y, 1)

            def dve_expert(dve, t, e):
                dve.wait_ge(s_exp_y, t * EXPERTS + e + 3)
                dve.wait_ge(s_acc, t * EXPERTS + e + 2)
                nc.vector.scalar_tensor_tensor(total, expert_p[e % 2], comb[:, e:e + 1], total,
                                               ALU.mult, ALU.add).then_inc(s_acc, 1)

            def act_store(act, t):
                act.wait_ge(s_acc, (t + 1) * EXPERTS + 2)
                act.dma_start(out[bass.ds(t * P, P), :], total).then_inc(s_store, 16)

            def dve_stored(dve, t):
                dve.wait_ge(s_store, t * 16 + 16)

            parts = Parts()
            parts.chain_restart = chain_restart
            parts.credits = credits
            parts.sp_load = sp_load
            parts.act_relu = act_relu
            parts.pe_rows = pe_rows
            parts.dve_residual = dve_residual
            parts.act_std = act_std
            parts.dve_normalise = dve_normalise
            parts.pe_y = pe_y
            parts.act_y_t = act_y_t
            parts.pe_logits = pe_logits
            parts.dve_logit_max = dve_logit_max
            parts.act_exp = act_exp
            parts.dve_combine = dve_combine
            parts.pe_combine_t = pe_combine_t
            parts.act_combine_t = act_combine_t
            parts.pe_bias = pe_bias
            parts.dve_total = dve_total
            parts.pe_hidden = pe_hidden
            parts.act_gelu = act_gelu
            parts.pe_expert = pe_expert
            parts.dve_expert = dve_expert
            parts.act_store = act_store
            parts.dve_stored = dve_stored
            return parts

        def second_table_alone():
            m_ = second_table()
            with nc.Block() as block:
                @block.sync
                def _(sp):
                    m_.sp_own(sp, 0, first=True)
                    with sp.Fori(1, TILES) as m:
                        m_.sp_own(sp, m)

                @block.scalar
                def _(act):
                    with act.Fori(0, TILES) as m:
                        m_.act_relu(act, m)
                        m_.act_row(act, m)
                        m_.act_stored(act, m)

                @block.vector
                def _(dve):
                    with dve.Fori(0, TILES) as m:
                        m_.dve_own(dve, m)
                        m_.dve_bias(dve, m)
                        m_.dve_self_loops(dve, m)

                @block.tensor
                def _(pe):
                    with pe.Fori(0, TILES) as m:
                        m_.pe_own(pe, m)
                        m_.pe_product(pe, m)
                        m_.pe_transpose(pe, m)
                        m_.pe_self_loops_done(pe, m)

        def nothing():
            pass

        def act_part_0(act, x_, m, later=nothing):
            x_.act_y_t(act, m)
            x_.act_exp(act, m)
            x_.act_gelu(act, m, 0)
            x_.act_gelu(act, m, 1)

        def act_part_1(act, x_, t, later=nothing):
            x_.act_combine_t(act, t)
            for e in (2, 3, 4):
                x_.act_gelu(act, t, e)

        def act_part_2(act, x_, t, m, later=nothing):
            if t is not None:
                x_.act_gelu(act, t, 5)
            later()
            if m is not None:
                x_.act_relu(act, m, first=t is None)
            if t is not None:
                x_.act_gelu(act, t, 6)
                x_.act_gelu(act, t, 7)
            if m is not None:
                x_.act_std(act, m)
            if t is not None:
                x_.act_store(act, t)

        def dve_part_0(dve, x_, m, later=nothing):
            later()
            x_.dve_logit_max(dve, m)
            x_.chain_restart(dve)
            x_.dve_combine(dve, m)

        def dve_part_1(dve, x_, t, later=nothing, first=False):
            x_.dve_total(dve, t, first)
            x_.dve_expert(dve, t, 0)
            later()
            x_.dve_expert(dve, t, 1)
            x_.dve_expert(dve, t, 2)

        def dve_part_2(dve, x_, t, m, later=nothing):
            if t is not None:
                x_.dve_expert(dve, t, 3)
            later()
            if t is not None:
                x_.dve_expert(dve, t, 4)
            if m is not None:
                x_.dve_residual(dve, m)
            if t is not None:
                for e in (5, 6, 7):
                    x_.dve_expert(dve, t, e)
            if m is not None:
                x_.dve_normalise(dve, m, first=t is None)

        def pe_part_0(pe, x_, m, later=nothing, first=False):
            x_.pe_y(pe, m, first)
            later()
            x_.pe_logits(pe, m)
            x_.pe_hidden(pe, m, 0)
            x_.pe_hidden(pe, m, 1)
            x_.pe_expert(pe, m, 0)

        def pe_part_1(pe, x_, t, later=nothing):
            x_.pe_combine_t(pe, t)
            x_.pe_hidden(pe, t, 2)
            x_.pe_bias(pe, t)
            later()
            x_.pe_expert(pe, t, 1)
            x_.pe_hidden(pe, t, 3)
            x_.pe_expert(pe, t, 2)
            x_.pe_hidden(pe, t, 4)

        def pe_part_2(pe, x_, t, m, later=nothing):
            if t is not None:
                x_.pe_expert(pe, t, 3)
            later()
            if t is not None:
                x_.pe_hidden(pe, t, 5)
                x_.pe_expert(pe, t, 4)
                x_.pe_hidden(pe, t, 6)
            if m is not None:
                x_.pe_rows(pe, m)
            if t is not None:
                x_.pe_expert(pe, t, 5)
                x_.pe_hidden(pe, t, 7)
                x_.pe_expert(pe, t, 6)
                x_.pe_expert(pe, t, 7)

        def dve_first_part_1(dve, x_, t, later=nothing):
            dve_part_1(dve, x_, t, later, first=True)

        def pe_first_part_0(pe, x_, m, later=nothing):
            pe_part_0(pe, x_, m, later, first=True)

        def experts_alone():
            x_ = expert_tiles()
            with nc.Block() as block:
                def tiles(eng, part_0, part_1, part_2, first_part_0, first_part_1):
                    part_2(eng, x_, None, 0)
                    first_part_0(eng, x_, 0)
                    first_part_1(eng, x_, 0)
                    part_2(eng, x_, 0, 1)
                    part_0(eng, x_, 1)
                    with eng.Fori(1, TILES - 1) as t:
                        part_1(eng, x_, t)
                        part_2(eng, x_, t, t + 1)
                        part_0(eng, x_, t + 1)
                    part_1(eng, x_, TILES - 1)
                    part_2(eng, x_, TILES - 1, None)

                @block.sync
                def _(sp):
                    x_.sp_load(sp, 0, first=True)
                    with sp.Fori(1, TILES) as m:
                        x_.sp_load(sp, m)

                @block.scalar
                def _(act):
                    tiles(act, act_part_0, act_part_1, act_part_2, act_part_0, act_part_1)

                @block.vector
                def _(dve):
                    tiles(dve, dve_part_0, dve_part_1, dve_part_2, dve_part_0, dve_first_part_1)
                    x_.dve_stored(dve, TILES - 1)

                @block.tensor
                def _(pe):
                    x_.credits(pe)
                    tiles(pe, pe_part_0, pe_part_1, pe_part_2, pe_first_part_0, pe_part_1)

        def group_number(it, j):
            return it * GROUPS_PER_STEP + j

        def first_layer_beside_table(e, next_layer):
            m_ = second_table()
            with nc.Block() as block:
                @block.sync
                def _(sp):
                    for it in range(2):
                        for j in range(GROUPS_PER_STEP):
                            e.sp_indices(sp, it, j, group_number(it, j))
                    m_.sp_own(sp, 0, first=True)
                    with sp.Fori(2, STEPS) as it:
                        e.sp_indices(sp, it, 0, group_number(it, 0))
                        e.sp_indices(sp, it, 1, group_number(it, 1))
                        m_.sp_own(sp, it - 1)
                        e.sp_indices(sp, it, 2, group_number(it, 2))
                    m_.sp_own(sp, TILES - 1)
                    for j in range(GROUPS_PER_STEP):
                        next_layer.sp_first_indices(sp, j)

                @block.gpsimd
                def _(pool):
                    with pool.Fori(0, STEPS) as it:
                        for j in range(GROUPS_PER_STEP):
                            e.pool_gather(pool, j, it)

                @block.vector
                def _(dve):
                    def group(it, j):
                        e.dve_place(dve, it, j + 1, group_number(it, j + 1))
                        e.dve_add(dve, it, j, group_number(it, j))

                    dve.wait_ge(s_weight, 16)
                    dve.sem_inc(e.s_add, 1)
                    e.dve_place(dve, 0, 0, 0)
                    for j in range(GROUPS_PER_STEP):
                        group(0, j)
                    with dve.Fori(1, STEPS) as it:
                        group(it, 0)
                        group(it, 1)
                        e.wait_added(dve, group_number(it, 1))
                        m_.dve_own(dve, it - 1)
                        m_.dve_bias(dve, it - 1)
                        m_.dve_self_loops(dve, it - 1)
                        group(it, 2)
                    e.wait_added(dve, GROUPS - 1)
                    m_.dve_own(dve, TILES - 1)
                    m_.dve_bias(dve, TILES - 1)
                    m_.dve_self_loops(dve, TILES - 1)

                @block.scalar
                def _(act):
                    for j in range(GROUPS_PER_STEP):
                        e.act_copy(act, j)
                    with act.Fori(1, STEPS) as it:
                        e.act_copy(act, group_number(it, 0))
                        e.act_copy(act, group_number(it, 1))
                        m_.act_relu(act, it - 1)
                        m_.act_row(act, it - 1)
                        m_.act_stored(act, it - 1)
                        e.act_copy(act, group_number(it, 2))
                    m_.act_relu(act, TILES - 1)
                    m_.act_row(act, TILES - 1)
                    m_.act_stored(act, TILES - 1)

                @block.tensor
                def _(pe):
                    def group(it, j):
                        e.pe_sum(pe, it, j, group_number(it, j))
                        e.pe_transpose(pe, group_number(it, j))

                    def row(m):
                        m_.pe_product(pe, m)
                        m_.pe_transpose(pe, m)
                        m_.pe_self_loops_done(pe, m)

                    pe.sem_inc(e.s_sum, GROUPS_PER_STEP)
                    for j in range(GROUPS_PER_STEP):
                        group(0, j)
                    with pe.Fori(1, STEPS) as it:
                        group(it, 0)
                        group(it, 1)
                        m_.pe_own(pe, it - 1)
                        row(it - 1)
                        group(it, 2)
                    m_.pe_own(pe, TILES - 1)
                    row(TILES - 1)

        def second_layer_beside_experts(e):
            x_ = expert_tiles()
            with nc.Block() as block:
                def steps(eng, start, end, part_0, part_1, part_2, first_part_0, first_part_1):
                    def with_group(it, j, part, *tiles):
                        start(it, j)
                        part(eng, x_, *tiles, lambda: end(it, j))

                    for j in range(GROUPS_PER_STEP):
                        start(0, j)
                        end(0, j)
                    start(1, 0)
                    end(1, 0)
                    with_group(1, 1, part_2, None, 0)
                    with_group(1, 2, first_part_0, 0)
                    with_group(2, 0, first_part_1, 0)
                    with_group(2, 1, part_2, 0, 1)
                    with_group(2, 2, part_0, 1)
                    with eng.Fori(3, STEPS) as it:
                        with_group(it, 0, part_1, it - 2)
                        with_group(it, 1, part_2, it - 2, it - 1)
                        with_group(it, 2, part_0, it - 1)
                    part_1(eng, x_, TILES - 2)
                    part_2(eng, x_, TILES - 2, TILES - 1, lambda: end(STEPS - 1, None))
                    part_0(eng, x_, TILES - 1)
                    part_1(eng, x_, TILES - 1)
                    part_2(eng, x_, TILES - 1, None)

                @block.sync
                def _(sp):
                    for j in range(GROUPS_PER_STEP):
                        e.sp_indices(sp, 1, j, group_number(1, j))
                    x_.sp_load(sp, 0, first=True)
                    with sp.Fori(2, STEPS) as it:
                        e.sp_indices(sp, it, 0, group_number(it, 0))
                        e.sp_indices(sp, it, 1, group_number(it, 1))
                        x_.sp_load(sp, it - 1)
                        e.sp_indices(sp, it, 2, group_number(it, 2))
                    x_.sp_load(sp, TILES - 1)

                @block.gpsimd
                def _(pool):
                    with pool.Fori(0, STEPS) as it:
                        for j in range(GROUPS_PER_STEP):
                            e.pool_gather(pool, j, it)

                @block.scalar
                def _(act):
                    def copy(it, j):
                        e.act_copy(act, group_number(it, j))

                    def wait_tile_summed(it, j):
                        if j == 1:
                            e.wait_added(act, group_number(it, 1))
                        if j is None:
                            e.wait_added(act, GROUPS - 1)

                    steps(act, copy, wait_tile_summed, act_part_0, act_part_1, act_part_2, act_part_0,
                          act_part_1)

                @block.vector
                def _(dve):
                    def place(it, j):
                        e.dve_place(dve, it, j + 1, group_number(it, j + 1))

                    def add(it, j):
                        if j is not None:
                            e.dve_add(dve, it, j, group_number(it, j))

                    dve.sem_inc(e.s_add, 1)
                    e.dve_place(dve, 0, 0, 0)
                    steps(dve, place, add, dve_part_0, dve_part_1, dve_part_2, dve_part_0, dve_first_part_1)
                    x_.dve_stored(dve, TILES - 1)

                @block.tensor
                def _(pe):
                    def summed(it, j):
                        e.pe_sum(pe, it, j, group_number(it, j))

                    def transpose(it, j):
                        if j is not None:
                            e.pe_transpose(pe, group_number(it, j))

                    pe.sem_inc(e.s_sum, GROUPS_PER_STEP)
                    x_.credits(pe)
                    steps(pe, summed, transpose, pe_part_0, pe_part_1, pe_part_2, pe_first_part_0, pe_part_1)

        write_first_table()
        with nc.If(spread == 1):
            layer_1 = edge_sums("layer_1", table_1, 0)
            layer_2 = edge_sums("layer_2", table_2, 1)
            first_layer_beside_table(layer_1, layer_2)
            second_layer_beside_experts(layer_2)
        with nc.Else():
            sum_edges_in_rounds("layer_1", table_1, 0, rounds)
            second_table_alone()
            sum_edges_in_rounds("layer_2", table_2, 1, rounds)
            experts_alone()


def lay_out(x, src, dst, edge_weight1, L0_gnn_W1, L0_gnn_b1, L0_gnn_W2, L0_gnn_b2,
           L0_ffn_router_w, L0_ffn_w1, L0_ffn_b1, L0_ffn_w2, L0_ffn_b2):
    import numpy as np

    def by_partition(edges, fill):
        flat = np.full(CHUNKS_PAD * P, fill, edges.dtype)
        flat[:N_EDGES] = edges
        return flat.reshape(CHUNKS_PAD, P).T

    x = np.asarray(x)
    x_pad = np.zeros((NODES, D), x.dtype)
    x_pad[:N_NODES] = x
    b1 = np.asarray(L0_ffn_b1).reshape(EXPERTS * HALF, P).T
    ins = {
        "x": x_pad,
        "src": by_partition(np.asarray(src), 0),
        "dst": by_partition(np.asarray(dst), N_NODES),
        "weight": by_partition(np.asarray(edge_weight1)[:, 0], 0),
        "gnn_w1": np.asarray(L0_gnn_W1).T, "gnn_b1": np.asarray(L0_gnn_b1),
        "gnn_w2": np.asarray(L0_gnn_W2).T, "gnn_b2": np.asarray(L0_gnn_b2),
        "router": np.asarray(L0_ffn_router_w).T,
        "moe_w1": np.asarray(L0_ffn_w1), "moe_b1": b1,
        "moe_w2": np.asarray(L0_ffn_w2), "moe_b2": np.asarray(L0_ffn_b2),
    }
    return {f"in_{n}": np.ascontiguousarray(a) for n, a in ins.items()}


def kernel(**inputs):
    import concourse.bacc as bacc
    from concourse.bass_utils import run_bass_kernel_spmd

    ins = lay_out(**inputs)
    nc = bacc.Bacc("TRN2", target_bir_lowering=False, num_devices=1)
    args = [nc.dram_tensor(n, a.shape, mybir.dt.from_np(a.dtype), kind="ExternalInput").ap() for n, a in ins.items()]
    out = nc.dram_tensor("out_rows", (NODES, D), F32, kind="ExternalOutput").ap()
    gnn_ffn_kernel(nc, *args, out)
    r = run_bass_kernel_spmd(nc, [ins], core_ids=[0])
    return r.results[0]["out_rows"][:N_NODES]
```
